# Optimizing a Trainium2 kernel written in Bass

```python
import numpy as np
import jax
import jax.numpy as jnp

def _softmax(x, axis=-1):
    return jax.nn.softmax(x, axis=axis)

def _gelu(x):
    return jax.nn.gelu(x, approximate=True)

def _silu(x):
    return jax.nn.silu(x)

def _sigmoid(x):
    return jax.nn.sigmoid(x)

def _layernorm(x, axis=-1, eps=1e-05):
    m = jnp.mean(x, axis=axis, keepdims=True)
    v = jnp.var(x, axis=axis, keepdims=True)
    return (x - m) / jnp.sqrt(v + eps)

def _scatter_add(tgt, idx, src, axis=0):
    return tgt.at[idx].add(src)

def _segment_sum(src, seg, n):
    return jax.ops.segment_sum(src, seg, n)
kernel_name = 'mk_xattn_ffn_d1_seqx_r8_d8a6bd'

def setup_inputs(seed: int=0):
    np.random.seed(seed)
    _w = jnp.asarray

    def _rec_inputs():
        import jax
        import jax.numpy as jnp
        _rk = jax.random.key(seed)
        x = 7.22e-05 + 1 * jax.random.normal(jax.random.fold_in(_rk, 1), (4, 512, 128), jnp.float32)
        _lenS = 512 - jax.random.randint(jax.random.fold_in(_rk, 7), (4,), 0, max(1, 512 // 4) + 1, jnp.int32)
        _lenS2 = 154 - jax.random.randint(jax.random.fold_in(_rk, 8), (4,), 0, max(1, 154 // 4) + 1, jnp.int32)
        _ctx_1024P = jax.random.normal(jax.random.fold_in(_rk, 11), (4, 16, 128), jnp.float32)
        _ctx_1024c = jax.random.dirichlet(jax.random.fold_in(_rk, 511), 0.3 * jnp.ones((16,), jnp.float32), (4, 154))
        _ctx_1024t = jnp.einsum('bsk,bkd->bsd', _ctx_1024c, _ctx_1024P)
        _ctx_1024t = _ctx_1024t * jax.lax.rsqrt(jnp.mean(jnp.square(_ctx_1024t)) + 1e-12) * 0.953939
        ctx_1024 = 4.13588e-05 + 0.999923 * (_ctx_1024t + 0.3 * jax.random.normal(jax.random.fold_in(_rk, 611), (4, 154, 128), jnp.float32))
        _validS = jnp.arange(512)[None, :] < _lenS[:, None]
        _validS2 = jnp.arange(154)[None, :] < _lenS2[:, None]
        _causal = jnp.tril(jnp.ones((512, 512), dtype=bool))
        mask_SxS2_ik0 = jnp.where(jnp.broadcast_to(_validS2[0:1, :], (512, 154)), 0, 1).astype(jnp.int32)
        return (x, ctx_1024, mask_SxS2_ik0)
    x, ctx_1024, mask_SxS2_ik0 = _rec_inputs()

    def _L0_xattn_setup():
        import jax, jax.numpy as jnp
        import numpy as np
        D_MODEL = 128
        N_HEADS = 16
        D_K = D_MODEL // N_HEADS
        B, L = (4, 256)
        key = jax.random.key(seed)
        ks = jax.random.split(key, 12)
        s_in = 1.0 / np.sqrt(D_MODEL)
        inp = {'Q': jax.random.normal(ks[0], (B, L, D_MODEL), jnp.float32), 'K': jax.random.normal(ks[1], (B, L, D_MODEL), jnp.float32), 'V': jax.random.normal(ks[2], (B, L, D_MODEL), jnp.float32), 'attn_mask': jnp.tril(jnp.ones((L, L), jnp.int32)), 'Wq': jax.random.normal(ks[3], (D_MODEL, D_MODEL), jnp.float32) * s_in, 'bq': jnp.zeros((D_MODEL,), jnp.float32), 'Wk': jax.random.normal(ks[4], (D_MODEL, D_MODEL), jnp.float32) * s_in, 'bk': jnp.zeros((D_MODEL,), jnp.float32), 'Wv': jax.random.normal(ks[5], (D_MODEL, D_MODEL), jnp.float32) * s_in, 'bv': jnp.zeros((D_MODEL,), jnp.float32), 'Wo': jax.random.normal(ks[6], (D_MODEL, D_MODEL), jnp.float32) * s_in, 'bo': jnp.zeros((D_MODEL,), jnp.float32)}
        return inp
    _L0_xattn_all = _L0_xattn_setup()
    _L0_xattn_in = {k: v for k, v in _L0_xattn_all.items() if k in ('Wq', 'bq', 'Wk', 'bk', 'Wv', 'bv', 'Wo', 'bo')}
    del _L0_xattn_all

    def _L0_ffn_setup():
        import jax, jax.numpy as jnp
        import numpy as np
        B, T, D = (2, 128, 128)
        E = 16
        H = 256
        K = 2
        HS = H * 2
        key = jax.random.key(seed)
        ks = jax.random.split(key, 16)
        s = 0.02
        f32 = jnp.float32
        return {'x': jax.random.normal(ks[0], (B, T, D), f32), 'Wg': jax.random.normal(ks[1], (D, E), f32) * s, 'W1': jax.random.normal(ks[2], (E, D, H), f32) * s, 'b1': jax.random.normal(ks[3], (E, H), f32) * s, 'W11': jax.random.normal(ks[4], (E, D, H), f32) * s, 'b11': jax.random.normal(ks[5], (E, H), f32) * s, 'W2': jax.random.normal(ks[6], (E, H, D), f32) * s, 'b2': jax.random.normal(ks[7], (E, D), f32) * s, 'Ws1': jax.random.normal(ks[8], (D, HS), f32) * s, 'bs1': jax.random.normal(ks[9], (HS,), f32) * s, 'Ws11': jax.random.normal(ks[10], (D, HS), f32) * s, 'bs11': jax.random.normal(ks[11], (HS,), f32) * s, 'Ws2': jax.random.normal(ks[12], (HS, D), f32) * s, 'bs2': jax.random.normal(ks[13], (D,), f32) * s}
    _L0_ffn_all = _L0_ffn_setup()
    _L0_ffn_in = {k: v for k, v in _L0_ffn_all.items() if k in ('Wg', 'W1', 'b1', 'W11', 'b11', 'W2', 'b2', 'Ws1', 'bs1', 'Ws11', 'bs11', 'Ws2', 'bs2')}
    del _L0_ffn_all
    return {'x': x, 'ctx_1024': ctx_1024, 'mask_SxS2_ik0': mask_SxS2_ik0, 'L0_xattn_Wq': _L0_xattn_in['Wq'], 'L0_xattn_bq': _L0_xattn_in['bq'], 'L0_xattn_Wk': _L0_xattn_in['Wk'], 'L0_xattn_bk': _L0_xattn_in['bk'], 'L0_xattn_Wv': _L0_xattn_in['Wv'], 'L0_xattn_bv': _L0_xattn_in['bv'], 'L0_xattn_Wo': _L0_xattn_in['Wo'], 'L0_xattn_bo': _L0_xattn_in['bo'], 'L0_ffn_Wg': _L0_ffn_in['Wg'], 'L0_ffn_W1': _L0_ffn_in['W1'], 'L0_ffn_b1': _L0_ffn_in['b1'], 'L0_ffn_W11': _L0_ffn_in['W11'], 'L0_ffn_b11': _L0_ffn_in['b11'], 'L0_ffn_W2': _L0_ffn_in['W2'], 'L0_ffn_b2': _L0_ffn_in['b2'], 'L0_ffn_Ws1': _L0_ffn_in['Ws1'], 'L0_ffn_bs1': _L0_ffn_in['bs1'], 'L0_ffn_Ws11': _L0_ffn_in['Ws11'], 'L0_ffn_bs11': _L0_ffn_in['bs11'], 'L0_ffn_Ws2': _L0_ffn_in['Ws2'], 'L0_ffn_bs2': _L0_ffn_in['bs2']}

def reference(x, ctx_1024, mask_SxS2_ik0, L0_xattn_Wq, L0_xattn_bq, L0_xattn_Wk, L0_xattn_bk, L0_xattn_Wv, L0_xattn_bv, L0_xattn_Wo, L0_xattn_bo, L0_ffn_Wg, L0_ffn_W1, L0_ffn_b1, L0_ffn_W11, L0_ffn_b11, L0_ffn_W2, L0_ffn_b2, L0_ffn_Ws1, L0_ffn_bs1, L0_ffn_Ws11, L0_ffn_bs11, L0_ffn_Ws2, L0_ffn_bs2):
    import jax
    import jax.numpy as jnp

    def _L0_xattn_ref(Q, K, V, Wq, bq, Wk, bk, Wv, bv, Wo, bo, attn_mask):
        import jax, jax.numpy as jnp
        import numpy as np
        D_MODEL = 128
        N_HEADS = 16
        D_K = D_MODEL // N_HEADS
        B, L = (4, 256)
        Bq, Lq, D = Q.shape
        Lk = K.shape[1]
        q = (Q @ Wq.T + bq).reshape(Bq, Lq, N_HEADS, D_K).transpose(0, 2, 1, 3)
        k = (K @ Wk.T + bk).reshape(Bq, Lk, N_HEADS, D_K).transpose(0, 2, 1, 3)
        v = (V @ Wv.T + bv).reshape(Bq, Lk, N_HEADS, D_K).transpose(0, 2, 1, 3)
        scores = jnp.einsum('bhqd,bhkd->bhqk', q, k) / jnp.sqrt(jnp.float32(D_K))
        mask = attn_mask[None, None, :, :]
        scores = jnp.where(mask == 0, jnp.float32(-jnp.inf), scores)
        attn = jax.nn.softmax(scores, axis=-1)
        out = jnp.einsum('bhqk,bhkd->bhqd', attn, v)
        out = out.transpose(0, 2, 1, 3).reshape(Bq, Lq, D)
        return out @ Wo.T + bo

    def _L0_ffn_ref(x, Wg, W1, b1, W11, b11, W2, b2, Ws1, bs1, Ws11, bs11, Ws2, bs2):
        import jax, jax.numpy as jnp
        import numpy as np
        B, T, D = (2, 128, 128)
        E = 16
        H = 256
        K = 2
        HS = H * 2
        b, t, d = x.shape
        xf = x.reshape(b * t, d)
        n = xf.shape[0]
        logits = xf @ Wg
        _, topi = jax.lax.top_k(logits, K)
        mask = jnp.zeros((n, E), bool).at[jnp.arange(n)[:, None], topi].set(True)
        gates = jax.nn.softmax(jnp.where(mask, logits, -jnp.inf), axis=-1)
        y = jnp.zeros_like(xf)
        for e in range(E):
            h = jax.nn.silu(xf @ W1[e] + b1[e]) * (xf @ W11[e] + b11[e])
            y = y + (h @ W2[e] + b2[e]) * gates[:, e, None]
        z = jax.nn.silu(xf @ Ws1 + bs1) * (xf @ Ws11 + bs11) @ Ws2 + bs2
        return (y + z).reshape(b, t, d)
    x = x + _L0_xattn_ref(_layernorm(x, axis=-1), ctx_1024, ctx_1024, L0_xattn_Wq, L0_xattn_bq, L0_xattn_Wk, L0_xattn_bk, L0_xattn_Wv, L0_xattn_bv, L0_xattn_Wo, L0_xattn_bo, mask_SxS2_ik0)
    x = x + _L0_ffn_ref(_layernorm(x, axis=-1), L0_ffn_Wg, L0_ffn_W1, L0_ffn_b1, L0_ffn_W11, L0_ffn_b11, L0_ffn_W2, L0_ffn_b2, L0_ffn_Ws1, L0_ffn_bs1, L0_ffn_Ws11, L0_ffn_bs11, L0_ffn_Ws2, L0_ffn_bs2)
    return x

_drawn_inputs = setup_inputs


def setup_inputs(seed=0):
    import zlib

    import numpy as np

    out = dict(_drawn_inputs(seed))
    spreads = {'L0_xattn_bq': (0.0, 0.301),
     'L0_xattn_bk': (0.0, 2.0),
     'L0_xattn_bv': (0.0, 0.1),
     'L0_xattn_bo': (0.0, 0.1)}
    factors = {'L0_ffn_Wg': 4.531,
     'L0_ffn_W1': 8.0,
     'L0_ffn_b1': 8.0,
     'L0_ffn_W11': 8.0,
     'L0_ffn_b11': 8.0,
     'L0_ffn_W2': 8.0,
     'L0_ffn_b2': 18.719,
     'L0_ffn_Ws1': 5.557,
     'L0_ffn_bs1': 8.0,
     'L0_ffn_Ws11': 5.548,
     'L0_ffn_bs11': 8.0,
     'L0_ffn_Ws2': 5.498,
     'L0_ffn_bs2': 13.423}
    for name, (base, spread) in spreads.items():
        noise = np.random.default_rng([zlib.crc32(name.encode()), seed]).standard_normal(out[name].shape)
        drawn = base * np.exp(spread * noise) if base else spread * noise
        out[name] = jnp.asarray(drawn.astype(out[name].dtype))
    for name, factor in factors.items():
        out[name] = (out[name] * factor).astype(out[name].dtype)
    return out
```

```python
from contextlib import ExitStack

import concourse.bass as bass
from concourse import mybir

ALU = mybir.AluOpType
ACT = mybir.ActivationFunctionType
AX = mybir.AxisListType
F32 = mybir.dt.float32
F32R = mybir.dt.float32r
F16 = mybir.dt.float16
BF16 = mybir.dt.bfloat16
I32 = mybir.dt.int32

P = 128
B, S, D = 4, 512, 128
NH, DK = 16, 8
SK = 154
SKP = 160
NG, HG = 4, 4
NE, H = 16, 256
NX = 18
NT = B * S // P
QT = S // P
TOK = B * S
EPS = 1e-5
MASKED = -float(2 ** 100)
BIG = 1e30

C_ID = 0
C_MQ = 128
C_MK = 129
C_SELM = 130
C_SELO = 134
C_EPS = 138
C_DESC = 139
C_END = 155
V_BQ, V_BK, V_B1, V_B11, V_BS2 = 0, 4, 8, 44, 80
V_END = 81
CW = SKP + P
WE = 2 * H + 2 * D
RP = 4
LAG = 4


class Chain:

    def __init__(self, eng, sem):
        self.eng, self.sem, self.base, self.i, self.per, self.k = eng, sem, 0, 0, 0, 0

    def then(self, ins):
        self.k += 1
        ins.then_inc(self.sem, 1)
        self.eng.wait_ge(self.sem, self.i * self.per + (self.base + self.k))

    def enter(self, i, per, first):
        self.base, self.i, self.per, self.k = self.base + self.k - first * per, i, per, 0

    def leave(self, end):
        assert self.k == self.per, (self.k, self.per)
        self.base, self.i, self.per, self.k = self.base + end * self.per, 0, 0, 0


def reach(eng, sem, i, per, k):
    if isinstance(i, int) and i * per + k <= 0:
        return
    eng.wait_ge(sem, i * per + k)


def first_of(i):
    return isinstance(i, int) and i == 0


def apart(eng, passed):
    eng.sem_inc(passed, 1)


def build(nc, x, ctx_t, wq, wk, wv, wo, mask_q, mask_k, mask_kl, bias_cols, bv_rows, bo_rows, wg, b2,
          w_ffn, consts, out):
    stack = ExitStack()
    with stack:
        def sb(name, shape, dt=F32):
            return stack.enter_context(nc.sbuf_tensor(name, shape, dt))

        def sem(name):
            return stack.enter_context(nc.semaphore(name))

        gate_dram = nc.dram_tensor("gate_rows", (NE, TOK), F32, kind="Internal").ap()
        cst = sb("cst", [P, C_END])
        vec = sb("vec", [P, V_END])
        bvr, bor = sb("bvr", [P, D]), sb("bor", [P, D])
        wgs, b2s = sb("wgs", [P, NE]), sb("b2s", [NE, D])
        wq_raw, wk_raw = sb("wq_raw", [P, NG * P]), sb("wk_raw", [P, NG * P])
        wv_raw, wo_s = sb("wv_raw", [P, D]), sb("wo_s", [P, D])
        ctx_s = sb("ctx_s", [P, B, CW])
        mq_raw, mk_raw, mkl_raw = sb("mq_raw", [P, QT, SK], I32), sb("mk_raw", [P, S], I32), sb("mkl_raw", [32, S], I32)
        xs = sb("xs", [P, NT, D])
        identb, repb = sb("identb", [P, P], BF16), sb("repb", [32, HG, 32], BF16)
        mq_b, mk_b, mkl_b = sb("mq_b", [P, QT, SK], BF16), sb("mk_b", [P, S], BF16), sb("mkl_b", [32, S], BF16)
        wq_hi, wq_lo = sb("wq_hi", [P, NG * P], F32R), sb("wq_lo", [P, NG * P], F32R)
        wk_hi, wk_lo = sb("wk_hi", [P, NG * P], F32R), sb("wk_lo", [P, NG * P], F32R)
        wv_hi, wv_lo = sb("wv_hi", [P, D], F32R), sb("wv_lo", [P, D], F32R)
        wg_hi, wg_lo = sb("wg_hi", [P, NE], F32R), sb("wg_lo", [P, NE], F32R)
        mbq, mbk = sb("mbq", [P, NG]), sb("mbk", [P, NG])
        key_on = sb("key_on", [P, QT, SK])
        row_any, row_inv, row_nan = sb("row_any", [P, QT]), sb("row_inv", [P, QT]), sb("row_nan", [P, QT])
        bn, mv = sb("bn", [P, NT, 6]), sb("mv", [P, NT, 2])
        std, rstd, nmr = sb("std", [P, NT]), sb("rstd", [P, NT]), sb("nmr", [P, NT])
        xn, x1 = sb("xn", [P, NT, D]), sb("x1", [P, NT, D])
        x_hi, x_lo = sb("x_hi", [P, TOK], F32R), sb("x_lo", [P, TOK], F32R)
        c_hi, c_lo = sb("c_hi", [P, CW], F32R), sb("c_lo", [P, CW], F32R)
        k_part, k_stack = sb("k_part", [P, NG, SKP]), sb("k_stack", [P, NG, SKP])
        ks, ksl = sb("ks", [P, NH, SKP], F32R), sb("ksl", [P, NG, HG, 32], F32R)
        v_all, v_part = sb("v_all", [P, 2, D]), sb("v_part", [P, 3, 2, D], BF16)
        vx, vl = sb("vx", [P, NH, 32], BF16), sb("vl", [P, NG, HG, 32], BF16)
        q_part, qs = sb("q_part", [P, 2, S]), sb("qs", [P, NG, S], F32R)
        mpad = sb("mpad", [P, 2, QT, P])
        pf = sb("pf", [P, RP, S])
        p_hi, p_lo = sb("p_hi", [P, RP, S], F16), sb("p_lo", [P, RP, S], F16)
        o_s = sb("o_s", [P, S])
        rinv, o_sum = sb("rinv", [P, QT, HG]), sb("o_sum", [P, QT, HG, DK])
        on, on_t = sb("on", [P, QT, D]), sb("on_t", [P, S])
        lg, top, one1, one2 = (sb(n, [P, NT, NE]) for n in ("lg", "top", "one1", "one2"))
        m1, m2, mi, g1, g2, ex = (sb(n, [P, NT]) for n in ("m1", "m2", "mi", "g1", "g2", "ex"))
        gt = xn[0:NE, :, :].rearrange("p t d -> p (t d)")
        w_raw = sb("w_raw", [P, 2, WE])
        w_hi = [sb(f"w_hi{i}", [P, WE], F32R) for i in range(2)]
        w_lo = [sb(f"w_lo{i}", [P, WE], F32R) for i in range(2)]
        gb = sb("gb", [P, 2, TOK])
        f_s, f_t, f_h = sb("f_s", [P, 2, S]), sb("f_t", [P, 2, S]), sb("f_h", [P, 4, S])
        h_hi, h_lo = sb("h_hi", [P, 4, S], F32R), sb("h_lo", [P, 4, S], F32R)
        yt = xs[:, :, :].rearrange("p t d -> p (t d)")

        ps = stack.enter_context(nc.psum_tensor("ps", [P, 8, 512], F32))
        Q_, M_, KS_, ST_, O_, T_ = 0, 1, 2, 4, 6, 7
        AB_ = 4

        (ld_x, ld_c, ld_w, ld_m, ld_ctx, dve_step, pool_passed, act_passed, cleared, consts_done, ln_var, ln_std, xn_done,
         xt_done, xhi_done, xlo_done, ctx_hi_done, ctx_split, k_mm, k_part_done, k_stack_done, ks_done, ksl_done, v_mm,
         v_done, vx_done, vl_done, q_mm, q_part_done, qs_done, smax_mm, max_done, mt_mm, qmax_done, st_mm, exp_done,
         phi_done, plo_done, pv_mm, os_done, ot_mm, on_done, ont_mm, ont_done, x1_mm, x1_done, lg_mm, ex_in,
         ex_done, gates_done, gt_mm, gt_done, gt_out, w_split, a_mm, b_mm, silu_done, t_done, h_done,
         hhi_done, hlo_done, w2_mm, y_mm, yt_done, ytt_mm, out_done, stored) = (sem(n) for n in (
            "ld_x ld_c ld_w ld_m ld_ctx dve_step pool_passed act_passed cleared consts_done ln_var ln_std xn_done "
            "xt_done xhi_done xlo_done ctx_hi_done ctx_split k_mm k_part_done k_stack_done ks_done ksl_done v_mm "
            "v_done vx_done vl_done q_mm q_part_done qs_done smax_mm max_done mt_mm qmax_done st_mm exp_done "
            "phi_done plo_done pv_mm os_done ot_mm on_done ont_mm ont_done x1_mm x1_done lg_mm ex_in "
            "ex_done gates_done gt_mm gt_done gt_out w_split a_mm b_mm silu_done t_done h_done "
            "hhi_done hlo_done w2_mm y_mm yt_done ytt_mm out_done stored").split())

        ld_f = [sem(f"ld_f{par}") for par in range(2)]
        ld_g = [sem(f"ld_g{par}") for par in range(2)]
        ident = cst[:, C_ID:C_ID + P]
        def k_psum(g):
            return ps[:, KS_ + g, 0:SKP]

        block = stack.enter_context(nc.Block())

        @block.sync
        def _(sp):
            sp.dma_start(xs[:, :, :], x).then_inc(ld_x, 16)
            sp.dma_start(cst[:, :], consts).then_inc(ld_c, 16)
            sp.dma_start(vec[:, :], bias_cols).then_inc(ld_c, 16)
            sp.dma_start(ctx_s[:, :, :], ctx_t).then_inc(ld_ctx, 16)
            for dst, src in ((wk_raw, wk), (wv_raw, wv), (wq_raw, wq), (wo_s, wo), (bvr, bv_rows), (bor, bo_rows),
                             (wgs, wg), (b2s, b2)):
                sp.dma_start(dst[:, :], src).then_inc(ld_w, 16)
            sp.dma_start(mq_raw[:, :, :], mask_q).then_inc(ld_m, 16)
            sp.dma_start(mk_raw[:, :], mask_k).then_inc(ld_m, 16)
            sp.dma_start(mkl_raw[:, :], mask_kl).then_inc(ld_m, 16)
            for e in range(2):
                sp.dma_start(w_raw[:, e, :], w_ffn[e, :, :]).then_inc(ld_f[e], 16)
            sp.wait_ge(gt_done, 4)
            sp.dma_start(gate_dram, gt[:, :]).then_inc(gt_out, 16)
            sp.wait_ge(gt_out, 16)
            with sp.Fori(1, NX // 2) as i:
                for par in range(2):
                    sp.wait_ge(w_split, i * 4 + (2 * par - 2))
                    sp.dma_start(w_raw[:, par, :],
                                 w_ffn[bass.ds(i * 2 + par, 1), :, :].rearrange("a p n -> (a p) n")).then_inc(ld_f[par], 16)
                    sp.wait_ge(h_done, i * 16 + (8 * par - 8))
                    sp.dma_start(gb[:, par, :],
                                 gate_dram[bass.ds(i * 2 + (par - 2), 1), :].rearrange("a n -> (a n)")
                                 .partition_broadcast(P)).then_inc(ld_g[par], 16)
            for t in range(B):
                sp.wait_ge(out_done, t + 1)
                sp.dma_start(out[:, QT * t:QT * t + QT, :], xn[:, QT * t:QT * t + QT, :]).then_inc(stored, 16)
            sp.wait_ge(stored, 16 * B)

        @block.vector
        def _(dve):
            chain = Chain(dve, dve_step)
            link = chain.then

            def norm(src, rnd):
                for t in range(NT):
                    last = dve.bn_stats(bn[:, t, :], src[:, t, :])
                link(last)
                for t in range(NT):
                    last = dve.bn_aggr(mv[:, t, :], bn[:, t, :])
                last.then_inc(ln_var, 1)
                dve.wait_ge(ln_std, rnd)
                link(dve.reciprocal(rstd[:, :], std[:, :]))
                link(dve.scalar_tensor_tensor(out=nmr[:, :], in0=mv[:, :, 0], scalar=-1.0, in1=rstd[:, :],
                                              op0=ALU.mult, op1=ALU.mult))
                for t in range(NT):
                    dve.tensor_scalar(xn[:, t, :], src[:, t, :], rstd[:, t:t + 1], nmr[:, t:t + 1],
                                      ALU.mult, ALU.add).then_inc(xn_done, 1)

            def split_x(rnd):
                for c in range(4):
                    dve.wait_ge(xhi_done, 4 * (rnd - 1) + c + 1)
                    dve.tensor_tensor(x_lo[:, c * S:(c + 1) * S], ps[:, c, :],
                                      x_hi[:, c * S:(c + 1) * S].bitcast(F32), ALU.subtract).then_inc(xlo_done, 1)

            dve.memset(mpad[:, :, :, :], 0.0)
            dve.memset(vx[:, :, :], 0.0)
            dve.memset(vl[:, :, :, :], 0.0)
            link(dve.memset(gb[:, :, :], 1.0))
            dve.memset(vx[:, :, 24:25], 1.0)
            for j in range(HG):
                last = dve.memset(vl[32 * j:32 * j + 32, :, j, 24:25], 1.0)
            last.then_inc(cleared, 1)
            dve.wait_ge(ld_x, 16)
            norm(xs, 1)
            dve.wait_ge(ld_c, 32)
            dve.wait_ge(ld_w, 128)
            dve.tensor_copy(identb[:, :], ident)
            dve.tensor_copy(repb[:, :, :], cst[0:32, 0:32].unsqueeze(1).to_broadcast([32, HG, 32]))
            dve.tensor_scalar(mbq[:, :], vec[:, V_BQ:V_BQ + NG], cst[:, C_MQ:C_MQ + 1], None, ALU.mult)
            dve.tensor_scalar(mbk[:, :], vec[:, V_BK:V_BK + NG], cst[:, C_MK:C_MK + 1], None, ALU.mult)
            weights = ((wk_hi, wk_lo, wk_raw), (wv_hi, wv_lo, wv_raw), (wq_hi, wq_lo, wq_raw), (wg_hi, wg_lo, wgs))
            for hi, _, raw in weights:
                last = dve.tensor_copy(hi[:, :], raw[:, :])
            link(last)
            for hi, lo, raw in weights:
                dve.tensor_tensor(lo[:, :], raw[:, :], hi[:, :].bitcast(F32), ALU.subtract)
            dve.wait_ge(ld_m, 48)
            for dst, src in ((mq_b[:, :, :], mq_raw[:, :, :]), (mk_b[:, :], mk_raw[:, :]), (mkl_b[:, :], mkl_raw[:, :])):
                dve.tensor_scalar(dst, src, 0.0, MASKED, ALU.is_equal, ALU.mult)
            link(dve.tensor_scalar(key_on[:, :, :], mq_raw[:, :, :], 0.0, None, ALU.not_equal))
            link(dve.tensor_reduce(row_any[:, :], key_on[:, :, :], AX.X, ALU.max))
            link(dve.reciprocal(row_inv[:, :], row_any[:, :]))
            link(dve.tensor_tensor(row_nan[:, :], row_any[:, :], row_inv[:, :], ALU.mult))
            link(dve.tensor_scalar(row_nan[:, :], row_nan[:, :], -1.0, None, ALU.add))
            for q in range(QT):
                rows = xs[:, :, :].rearrange("p (b q) d -> p b q d", q=QT)[:, :, q, :]
                last = dve.scalar_tensor_tensor(out=rows, in0=rows, scalar=row_nan[:, q:q + 1],
                                                in1=bor[:, :].unsqueeze(1).to_broadcast([P, B, D]),
                                                op0=ALU.add, op1=ALU.add)
            last.then_inc(consts_done, 1)
            split_x(1)

            def q_stack(b, g):
                reach(dve, q_part_done, b, 4, g + 1)
                dve.scalar_tensor_tensor(out=qs[:, g, :], in0=ps[:, Q_, :], scalar=vec[:, V_BQ + g:V_BQ + g + 1],
                                         in1=q_part[:, g % 2, :], op0=ALU.add,
                                         op1=ALU.subtract).then_inc(qs_done, 1)

            def row_max(b, g, q):
                reach(dve, smax_mm, b, 16, 4 * g + q + 1)
                dve.tensor_reduce(mpad[:, g % 2, q, 96:96 + HG].rearrange("p (a c) -> p a c", a=2),
                                  ps[:, KS_:KS_ + 2, 0:2 * SK].rearrange("p a (c k) -> p a c k", c=2),
                                  AX.X, ALU.max, negate=True).then_inc(max_done, 1)

            def p_low(b, g, t):
                n = 5 * g + t
                reach(dve, phi_done, b, 20, n + 1)
                dve.tensor_tensor(p_lo[:, n % RP, :], pf[:, n % RP, :], p_hi[:, n % RP, :],
                                  ALU.subtract).then_inc(plo_done, 1)

            def normalize(b, g):
                reach(dve, ot_mm, b, 4, g + 1)
                o = ps[:, T_, :].rearrange("p (q j c) -> p q j c", q=QT, j=HG)
                dve.reciprocal(rinv[:, :, :], o[:, :, :, 24])
                link(dve.tensor_reduce(o_sum[:, :, :, :].rearrange("p q j d -> p (q j) d"),
                                       ps[:, T_, :].rearrange("p (a c) -> p a c", c=32)[:, :, 0:24]
                                       .rearrange("p a (t d) -> p a d t", d=DK), AX.X, ALU.add))
                dve.tensor_tensor(on[:, :, 32 * g:32 * g + 32].rearrange("p q (j d) -> p q j d", d=DK),
                                  o_sum[:, :, :, :],
                                  rinv[:, :, :].unsqueeze(3).to_broadcast([P, QT, HG, DK]),
                                  ALU.mult).then_inc(on_done, 1)

            def batch(b):
                chain.enter(b, 9, 0 if isinstance(b, int) else 1)
                reach(dve, ctx_hi_done, b, 1, 1)
                dve.tensor_tensor(c_lo[:, :], ctx_s[:, bass.ds(b, 1), :].rearrange("p a n -> p (a n)"),
                                  c_hi[:, :].bitcast(F32), ALU.subtract).then_inc(ctx_split, 1)
                for g in range(NG):
                    reach(dve, k_part_done, b, 4, g + 1)
                    reach(dve, ks_done, b, 16, 4 * g + 4 - 16)
                    dve.scalar_tensor_tensor(out=k_stack[:, g, :], in0=k_psum(g), scalar=vec[:, V_BK + g:V_BK + g + 1],
                                             in1=k_part[:, g, :], op0=ALU.add,
                                             op1=ALU.subtract).then_inc(k_stack_done, 1)
                reach(dve, v_mm, b, 1, 1)
                reach(dve, vx_done, b, 1, 0)
                link(dve.tensor_tensor(v_all[:, :, :], ps[:, M_, 0:2 * D].rearrange("p (a n) -> p a n", a=2),
                                       bvr[:, :].unsqueeze(1).to_broadcast([P, 2, D]), ALU.add))
                for part in range(2):
                    link(dve.tensor_copy(v_part[:, part, :, :], v_all[:, :, :]))
                    link(dve.tensor_tensor(v_all[:, :, :], v_all[:, :, :], v_part[:, part, :, :], ALU.subtract))
                dve.tensor_copy(v_part[:, 2, :, :], v_all[:, :, :]).then_inc(v_done, 1)
                reach(dve, v_done, b, 1, 1)
                reach(dve, pv_mm, b, 20, 0)
                for j in range(HG):
                    q = slice(32 * j, 32 * j + 32)
                    last = dve.tensor_copy(vl[q, :, j, 0:3 * DK].rearrange("p g (t d) -> p g t d", d=DK),
                                           v_part[q, :, 1, :].rearrange("p t (g j d) -> p g j t d", g=NG, j=HG)[:, :, j, :, :])
                last.then_inc(vl_done, 1)
                q_stack(b, 0)
                for q in range(QT):
                    row_max(b, 0, q)
                for g in range(NG):
                    if g + 1 < NG:
                        q_stack(b, g + 1)
                    for t in range(5):
                        if g + 1 < NG and t < QT:
                            row_max(b, g + 1, t)
                        p_low(b, g, t)
                    normalize(b, g)
                reach(dve, x1_mm, b, 1, 1)
                tiles = bass.ds(b * QT, QT)
                dve.tensor_tensor(x1[:, tiles, :], ps[:, T_, :].rearrange("p (q d) -> p q d", q=QT), xs[:, tiles, :],
                                  ALU.add).then_inc(x1_done, 1)

            batch(0)
            chain.leave(1)
            with dve.Fori(1, B) as b:
                batch(b)
            chain.leave(B)

            dve.wait_ge(x1_done, B)
            norm(x1, 2)
            split_x(2)
            dve.wait_ge(lg_mm, 1)
            link(dve.tensor_copy(lg[:, :, :], ps[:, AB_, 0:NT * NE].rearrange("p (t e) -> p t e", e=NE)))

            def row(v):
                return v[:, :].unsqueeze(2).to_broadcast([P, NT, NE])

            desc = cst[:, C_DESC:C_DESC + NE].unsqueeze(1).to_broadcast([P, NT, NE])

            def first_max(of, m, one):
                link(dve.tensor_reduce(m[:, :], of[:, :, :], AX.X, ALU.max))
                link(dve.tensor_tensor(one[:, :, :], of[:, :, :], row(m), ALU.is_equal))
                link(dve.tensor_tensor(one[:, :, :], one[:, :, :], desc, ALU.mult))
                link(dve.tensor_reduce(mi[:, :], one[:, :, :], AX.X, ALU.max))
                link(dve.tensor_tensor(one[:, :, :], row(mi), desc, ALU.is_equal))

            first_max(lg, m1, one1)
            link(dve.scalar_tensor_tensor(out=top[:, :, :], in0=one1[:, :, :], scalar=-BIG, in1=lg[:, :, :],
                                          op0=ALU.mult, op1=ALU.add))
            first_max(top, m2, one2)
            dve.tensor_tensor(m2[:, :], m2[:, :], m1[:, :], ALU.subtract).then_inc(ex_in, 1)
            dve.wait_ge(ex_done, 1)
            link(dve.tensor_scalar(g2[:, :], ex[:, :], 1.0, None, ALU.add))
            link(dve.reciprocal(g1[:, :], g2[:, :]))
            link(dve.tensor_tensor(g2[:, :], g1[:, :], ex[:, :], ALU.mult))
            link(dve.tensor_tensor(one1[:, :, :], one1[:, :, :], row(g1), ALU.mult))
            link(dve.tensor_tensor(one2[:, :, :], one2[:, :, :], row(g2), ALU.mult))
            dve.tensor_tensor(lg[:, :, :], one1[:, :, :], one2[:, :, :], ALU.add).then_inc(gates_done, 1)

            def linear_half(i, k):
                e, c = i * 2 + k // 8, k % 2
                reach(dve, b_mm, i, 16, k + 1)
                reach(dve, silu_done, i, 16, k + 1)
                reach(dve, h_done, i, 16, k - 1)
                dve.scalar_tensor_tensor(out=f_t[:, k % 2, :], in0=ps[:, AB_ + 2 * (k % 2) + 1, :],
                                         scalar=vec[:, bass.ds(e * 2 + (V_B11 + c), 1)], in1=f_s[:, k % 2, :],
                                         op0=ALU.add, op1=ALU.mult).then_inc(t_done, 1)

            def h_low(i, k):
                reach(dve, hhi_done, i, 16, k + 1)
                reach(dve, w2_mm, i, 16, k - 3)
                dve.tensor_tensor(h_lo[:, k % 4, :], f_h[:, k % 4, :], h_hi[:, k % 4, :].bitcast(F32),
                                  ALU.subtract).then_inc(hlo_done, 1)

            def experts(i):
                for k in range(16):
                    linear_half(i, k)
                    if k >= 2 or not first_of(i):
                        h_low(i, k - 2)

            experts(0)
            with dve.Fori(1, NX // 2) as i:
                experts(i)
            for k in (14, 15):
                h_low(NX // 2 - 1, k)
            for t in range(B):
                dve.wait_ge(ytt_mm, t + 1)
                dve.tensor_tensor(xn[:, QT * t:QT * t + QT, :], ps[:, AB_ + t, :].rearrange("p (q d) -> p q d", q=QT),
                                  x1[:, QT * t:QT * t + QT, :], ALU.add).then_inc(out_done, 1)

        @block.gpsimd
        def _(pool):
            def batch(b):
                for g in range(NG):
                    reach(pool, k_stack_done, b, 4, g + 1)
                    reach(pool, st_mm, b, 20, 5 * g + 5 - 20)
                    apart(pool, pool_passed)
                    for j in range(HG):
                        pool.tensor_scalar(ks[:, HG * g + j, :], k_stack[:, g, :], cst[:, C_SELM + j:C_SELM + j + 1],
                                           cst[:, C_SELO + j:C_SELO + j + 1], ALU.mult, ALU.add).then_inc(ks_done, 1)
                    reach(pool, ks_done, b, 16, 4 * g + 4)
                    apart(pool, pool_passed)
                    pool.tensor_copy(ksl[:, g, :, :], ks[:, HG * g:HG * g + HG, P:SKP].bitcast(F32)).then_inc(ksl_done, 1)
                reach(pool, v_done, b, 1, 1)
                reach(pool, pv_mm, b, 20, 0)
                apart(pool, pool_passed)
                pool.tensor_copy(vx[:, :, 0:3 * DK].rearrange("p h (t d) -> p h t d", d=DK),
                                 v_part[:, :, 0, :].rearrange("p t (h d) -> p h t d", d=DK)).then_inc(vx_done, 1)
                for n in range(20):
                    reach(pool, exp_done, b, 20, n + 1)
                    reach(pool, pv_mm, b, 20, n + 1 - RP)
                    apart(pool, pool_passed)
                    pool.tensor_copy(p_hi[:, n % RP, :], pf[:, n % RP, :]).then_inc(phi_done, 1)

            def split_weights(i, par):
                reach(pool, ld_f[par], i, 16, 16)
                reach(pool, w2_mm, i, 16, 8 * par - 8)
                apart(pool, pool_passed)
                pool.tensor_copy(w_hi[par][:, :], w_raw[:, par, :]).then_inc(w_split, 1)
                reach(pool, w_split, i, 4, 2 * par + 1)
                pool.tensor_tensor(w_lo[par][:, :], w_raw[:, par, :], w_hi[par][:, :].bitcast(F32),
                                   ALU.subtract).then_inc(w_split, 1)

            def gate(i, k):
                if k % 8 == 0 and not first_of(i):
                    pool.wait_ge(ld_g[k // 8], i * 16)
                reach(pool, t_done, i, 16, k + 1)
                reach(pool, hlo_done, i, 16, k - 3)
                pool.tensor_tensor(f_h[:, k % 4, :], f_t[:, k % 2, :],
                                   gb[:, k // 8, (k % 8) // 2 * S:(k % 8) // 2 * S + S], ALU.mult).then_inc(h_done, 1)

            pool.wait_ge(cleared, 1)
            pool.wait_ge(ld_c, 32)
            batch(0)
            with pool.Fori(1, B) as b:
                batch(b)
            split_weights(0, 0)
            split_weights(0, 1)

            def experts(i, last=False):
                for k in range(16):
                    gate(i, k)
                    if k == LAG and not first_of(i):
                        split_weights(i, 1)
                    if k == 8 + LAG and not last:
                        split_weights(i + 1, 0)

            experts(0)
            with pool.Fori(1, NX // 2 - 1) as i:
                experts(i)
            experts(NX // 2 - 1, last=True)

        @block.scalar
        def _(act):
            def std_dev(rnd):
                act.wait_ge(ln_var, rnd)
                act.activation(std[:, :], mv[:, :, 1], ACT.Sqrt, bias=cst[:, C_EPS:C_EPS + 1]).then_inc(ln_std, 1)

            def x_high(rnd):
                for c in range(4):
                    act.wait_ge(xt_done, 4 * (rnd - 1) + c + 1)
                    act.activation(x_hi[:, c * S:(c + 1) * S], ps[:, c, :], ACT.Copy).then_inc(xhi_done, 1)

            act.wait_ge(ld_c, 32)
            std_dev(1)
            x_high(1)
            act.wait_ge(consts_done, 1)
            act.wait_ge(ld_ctx, 16)

            def q_hi(b, g):
                reach(act, q_mm, b, 4, g + 1)
                reach(act, qs_done, b, 4, g - 1)
                act.activation(q_part[:, g % 2, :], ps[:, Q_, :], ACT.Identity, bias=mbq[:, g:g + 1],
                               scale=cst[:, C_MQ:C_MQ + 1]).then_inc(q_part_done, 1)

            def q_max_rows(b, g):
                reach(act, mt_mm, b, 4, g + 1)
                act.activation(qs[96:128, g, :], ps[96:128, M_, :], ACT.Copy).then_inc(qmax_done, 1)

            def batch(b):
                reach(act, v_mm, b, 1, 0)
                apart(act, act_passed)
                act.activation(c_hi[:, :], ctx_s[:, bass.ds(b, 1), :].rearrange("p a n -> p (a n)"),
                               ACT.Copy).then_inc(ctx_hi_done, 1)
                for g in range(NG):
                    reach(act, k_mm, b, 4, g + 1)
                    reach(act, k_stack_done, b, 4, g + 1 - 4)
                    act.activation(k_part[:, g, :], k_psum(g), ACT.Identity, bias=mbk[:, g:g + 1],
                                   scale=cst[:, C_MK:C_MK + 1]).then_inc(k_part_done, 1)
                q_hi(b, 0)
                q_max_rows(b, 0)
                for g in range(NG):
                    if g + 1 < NG:
                        q_hi(b, g + 1)
                    for t in range(5):
                        n = 5 * g + t
                        reach(act, st_mm, b, 20, n + 1)
                        reach(act, plo_done, b, 20, n + 1 - RP)
                        act.activation(pf[:, n % RP, :], ps[:, ST_ + n % 2, :], ACT.Exp,
                                       scale=DK ** -0.5).then_inc(exp_done, 1)
                    if g + 1 < NG:
                        q_max_rows(b, g + 1)
                    reach(act, pv_mm, b, 20, 5 * g + 5)
                    reach(act, ot_mm, b, 4, g)
                    act.activation(o_s[:, :], ps[:, O_, :], ACT.Copy).then_inc(os_done, 1)
                reach(act, ont_mm, b, 1, 1)
                reach(act, x1_mm, b, 1, 0)
                act.activation(on_t[:, :], ps[:, T_, :], ACT.Copy).then_inc(ont_done, 1)

            batch(0)
            with act.Fori(1, B) as b:
                batch(b)
            std_dev(2)
            x_high(2)
            act.wait_ge(ex_in, 1)
            act.activation(ex[:, :], m2[:, :], ACT.Exp).then_inc(ex_done, 1)
            for c in range(4):
                act.wait_ge(gt_mm, c + 1)
                act.activation(gt[:, c * S:(c + 1) * S], ps[0:NE, c, :], ACT.Copy).then_inc(gt_done, 1)

            def silu(i, k):
                e, c = i * 2 + k // 8, k % 2
                reach(act, a_mm, i, 16, k + 1)
                reach(act, t_done, i, 16, k - 1)
                apart(act, act_passed)
                act.activation(f_s[:, k % 2, :], ps[:, AB_ + 2 * (k % 2), :], ACT.Silu,
                               bias=vec[:, bass.ds(e * 2 + (V_B1 + c), 1)]).then_inc(silu_done, 1)

            def h_high(i, k):
                reach(act, h_done, i, 16, k + 1)
                reach(act, w2_mm, i, 16, k - 3)
                act.activation(h_hi[:, k % 4, :], f_h[:, k % 4, :], ACT.Copy).then_inc(hhi_done, 1)

            def experts(i):
                for k in range(16):
                    silu(i, k)
                    if k >= 2 or not first_of(i):
                        h_high(i, k - 2)

            experts(0)
            with act.Fori(1, NX // 2) as i:
                experts(i)
            for k in (14, 15):
                h_high(NX // 2 - 1, k)
            for c in range(B):
                act.wait_ge(y_mm, c + 1)
                act.activation(yt[:, c * S:(c + 1) * S], ps[:, c, :], ACT.Identity,
                               bias=vec[:, V_BS2:V_BS2 + 1]).then_inc(yt_done, 1)

        @block.tensor
        def _(pe):
            def split_mm(out_ap, w_hi_ap, w_lo_ap, m_hi_ap, m_lo_ap, start=True, stop=True):
                pe.matmul(out_ap, w_hi_ap, m_hi_ap, start=start, stop=False)
                pe.matmul(out_ap, w_hi_ap, m_lo_ap, start=False, stop=False)
                return pe.matmul(out_ap, w_lo_ap, m_hi_ap, start=False, stop=stop)

            def turn_tokens(rnd):
                for t in range(NT):
                    pe.wait_ge(xn_done, NT * (rnd - 1) + t + 1)
                    last = pe.transpose(ps[:, t // 4, (t % 4) * P:(t % 4 + 1) * P], xn[:, t, :], ident)
                    if t % 4 == 3:
                        last.then_inc(xt_done, 1)

            pe.wait_ge(ld_c, 32)
            turn_tokens(1)
            pe.wait_ge(xlo_done, 4)

            def queries(b, g):
                reach(pe, qs_done, b, 4, g)
                tok = bass.ds(b * S, S)
                w = slice(P * g, P * g + P)
                split_mm(ps[:, Q_, :], wq_hi[:, w], wq_lo[:, w], x_hi[:, tok], x_lo[:, tok]).then_inc(q_mm, 1)

            def score_rows(b, g, q):
                reach(pe, qs_done, b, 4, g + 1)
                reach(pe, ks_done, b, 16, 4 * g + 4)
                reach(pe, max_done, b, 16, 4 * g + q)
                for a in range(2):
                    o = ps[:, KS_ + a, 0:2 * SK].rearrange("p (c k) -> p c k", c=2)
                    pe.matmul(o, identb[:, :], mq_b[:, q:q + 1, :].to_broadcast([P, 2, SK]), start=True, stop=False)
                    last = pe.matmul(o, qs[0:96, g, P * q:P * q + P], ks[0:96, HG * g + 2 * a:HG * g + 2 * a + 2, 0:SK],
                                     start=False, stop=True)
                last.then_inc(smax_mm, 1)

            def turn_max(b, g):
                reach(pe, max_done, b, 16, 4 * g + 4)
                reach(pe, qmax_done, b, 4, g)
                reach(pe, v_done, b, 1, 1)
                for q in range(QT):
                    last = pe.transpose(ps[:, M_, P * q:P * q + P], mpad[:, g % 2, q, :], ident)
                last.then_inc(mt_mm, 1)

            def scores(b, g, t):
                n = 5 * g + t
                if t == 0:
                    reach(pe, qmax_done, b, 4, g + 1)
                reach(pe, exp_done, b, 20, n - 1)
                o = ps[:, ST_ + n % 2, :]
                if t == 0:
                    pe.matmul(o, repb[:, :, :], mkl_b[:, :], start=True, stop=False)
                    reach(pe, ksl_done, b, 4, g + 1)
                    lhs = ksl[:, g, :, :]
                else:
                    pe.matmul(o, identb[:, :], mk_b[:, :], start=True, stop=False)
                    lhs = ks[:, HG * g + t - 1, 0:P]
                pe.matmul(o, lhs, qs[:, g, :], start=False, stop=True).then_inc(st_mm, 1)

            def weighted(b, g, t):
                n = 5 * g + t
                if t == 0:
                    reach(pe, os_done, b, 4, g)
                    reach(pe, vx_done, b, 1, 1)
                    reach(pe, vl_done, b, 1, 1)
                reach(pe, plo_done, b, 20, n + 1)
                for p in (p_hi, p_lo):
                    if t == 0:
                        last = pe.matmul(ps[:, O_, :], vl[:, g, :, :], p[:, n % RP, :], start=(p is p_hi), stop=False,
                                         skip_group_check=True)
                    else:
                        j = t - 1
                        last = pe.matmul(ps[32 * j:32 * j + 32, O_, :], vx[:, HG * g + j, :], p[:, n % RP, :],
                                         start=False, stop=(p is p_lo), skip_group_check=True)
                last.then_inc(pv_mm, 1)

            def turn_out(b, g):
                reach(pe, os_done, b, 4, g + 1)
                if g == 0:
                    reach(pe, x1_done, b, 1, 0)
                else:
                    reach(pe, on_done, b, 4, g)
                for q in range(QT):
                    last = pe.transpose(ps[:, T_, P * q:P * q + P], o_s[:, P * q:P * q + P], ident)
                last.then_inc(ot_mm, 1)

            def batch(b):
                reach(pe, ctx_split, b, 1, 1)
                reach(pe, max_done, b, 16, 0)
                reach(pe, exp_done, b, 20, 0)
                for g in range(NG):
                    w = slice(P * g, P * g + P)
                    split_mm(k_psum(g), wk_hi[:, w], wk_lo[:, w], c_hi[:, 0:SKP], c_lo[:, 0:SKP]).then_inc(k_mm, 1)
                reach(pe, qmax_done, b, 4, 0)
                for a, w in enumerate((slice(0, P), slice(SKP, SKP + P))):
                    last = split_mm(ps[:, M_, D * a:D * a + D], c_hi[:, w], c_lo[:, w], wv_hi[:, :], wv_lo[:, :])
                last.then_inc(v_mm, 1)
                queries(b, 0)
                reach(pe, k_stack_done, b, 4, 4)
                for q in range(QT):
                    score_rows(b, 0, q)
                turn_max(b, 0)
                for g in range(NG):
                    more = g + 1 < NG
                    if more:
                        queries(b, g + 1)
                    scores(b, g, 0)
                    scores(b, g, 1)
                    for t in range(5):
                        if more and t < QT:
                            score_rows(b, g + 1, t)
                        if t + 2 < 5:
                            scores(b, g, t + 2)
                        weighted(b, g, t)
                    if more:
                        turn_max(b, g + 1)
                    turn_out(b, g)
                reach(pe, on_done, b, 4, 4)
                for q in range(QT):
                    last = pe.transpose(ps[:, T_, P * q:P * q + P], on[:, q, :], ident)
                last.then_inc(ont_mm, 1)
                reach(pe, ont_done, b, 1, 1)
                for q in range(QT):
                    last = pe.matmul(ps[:, T_, P * q:P * q + P], on_t[:, P * q:P * q + P], wo_s[:, :],
                                     start=True, stop=True)
                last.then_inc(x1_mm, 1)

            pe.wait_ge(consts_done, 1)
            batch(0)
            with pe.Fori(1, B) as b:
                batch(b)

            turn_tokens(2)
            pe.wait_ge(xlo_done, 8)
            for t in range(NT):
                w = slice(P * t, P * t + P)
                last = split_mm(ps[:, AB_, NE * t:NE * t + NE], x_hi[:, w], x_lo[:, w], wg_hi[:, :], wg_lo[:, :])
            last.then_inc(lg_mm, 1)
            pe.wait_ge(gates_done, 1)
            for t in range(NT):
                last = pe.transpose(ps[0:NE, t // 4, (t % 4) * P:(t % 4 + 1) * P], lg[:, t, :], ident)
                if t % 4 == 3:
                    last.then_inc(gt_mm, 1)
            pe.wait_ge(gt_done, 4)

            def first(i, k):
                if k % 8 == 0:
                    reach(pe, w_split, i, 4, 2 * (k // 8) + 2)
                reach(pe, silu_done, i, 16, k - 1)
                reach(pe, t_done, i, 16, k - 1)
                hi, lo = w_hi[k // 8], w_lo[k // 8]
                tok = slice((k % 8) // 2 * S, (k % 8) // 2 * S + S)
                for m, done in ((0, a_mm), (1, b_mm)):
                    w = slice(H * m + P * (k % 2), H * m + P * (k % 2) + P)
                    split_mm(ps[:, AB_ + 2 * (k % 2) + m, :], hi[:, w], lo[:, w], x_hi[:, tok],
                             x_lo[:, tok]).then_inc(done, 1)

            def second(i, k):
                k16 = k % 16
                reach(pe, hlo_done, i, 16, k + 1)
                hi, lo = w_hi[k16 // 8], w_lo[k16 // 8]
                w = slice(2 * H + P * (k % 2), 2 * H + P * (k % 2) + P)
                blk = (k16 % 8) // 2
                start = first_of(i) and k in (0, 2, 4, 6)
                o = ps[:, blk, :]
                pe.matmul(o, hi[:, w], h_hi[:, k % 4, :], start=start, stop=False, skip_group_check=True)
                pe.matmul(o, hi[:, w], h_lo[:, k % 4, :], start=False, stop=False, skip_group_check=True)
                pe.matmul(o, lo[:, w], h_hi[:, k % 4, :], start=False, stop=False,
                          skip_group_check=True).then_inc(w2_mm, 1)

            def experts(i):
                for k in range(16):
                    first(i, k)
                    if k >= LAG or not first_of(i):
                        second(i, k - LAG)

            experts(0)
            with pe.Fori(1, NX // 2) as i:
                experts(i)
            for k in range(16 - LAG, 16):
                second(NX // 2 - 1, k)
            for c in range(B):
                pe.matmul(ps[:, c, :], b2s[:, :], gt[:, c * S:(c + 1) * S], start=False, stop=True,
                          skip_group_check=True).then_inc(y_mm, 1)
            for c in range(B):
                pe.wait_ge(yt_done, c + 1)
                for q in range(QT):
                    last = pe.transpose(ps[:, AB_ + c, P * q:P * q + P], yt[:, S * c + P * q:S * c + P * q + P], ident)
                last.then_inc(ytt_mm, 1)


def constants():
    import numpy as np
    c = np.zeros((P, C_END), np.float32)
    p = np.arange(P)
    c[:, C_ID:C_ID + P] = np.eye(P)
    c[:, C_MQ] = p // 32 == 1
    c[:, C_MK] = p // 32 == 2
    for j in range(HG):
        c[:, C_SELM + j] = (p < 96) & ((p % 32) // DK == j)
        c[:, C_SELO + j] = p == 96 + j
    c[:, C_EPS] = EPS
    c[:, C_DESC:C_DESC + NE] = NE - np.arange(NE)
    return c


def kernel(x, ctx_1024, mask_SxS2_ik0, L0_xattn_Wq, L0_xattn_bq, L0_xattn_Wk, L0_xattn_bk, L0_xattn_Wv, L0_xattn_bv,
           L0_xattn_Wo, L0_xattn_bo, L0_ffn_Wg, L0_ffn_W1, L0_ffn_b1, L0_ffn_W11, L0_ffn_b11, L0_ffn_W2, L0_ffn_b2,
           L0_ffn_Ws1, L0_ffn_bs1, L0_ffn_Ws11, L0_ffn_bs11, L0_ffn_Ws2, L0_ffn_bs2):
    import numpy as np
    import concourse.bacc as bacc
    from concourse.bass_utils import run_bass_kernel_spmd

    def stacked(w):
        return np.tile(np.asarray(w).T.reshape(D, NG, 1, 32), (1, 1, 4, 1)).reshape(D, NG * P)

    def stacked_bias(v):
        return np.tile(np.asarray(v).reshape(NG, 1, 32), (1, 4, 1)).reshape(NG, P).T

    def halves(w):
        return np.stack([w[..., 0:H], w[..., H:2 * H]])

    ctx_t = np.zeros((D, B, CW), np.float32)
    c = np.asarray(ctx_1024).transpose(2, 0, 1)
    ctx_t[:, :, 0:SK] = c
    for j in range(HG):
        ctx_t[:, :, SKP + 32 * j:SKP + 32 * j + SK - P] = c[:, :, P:SK]
    mask = np.asarray(mask_SxS2_ik0)
    mask_kl = np.zeros((32, S), mask.dtype)
    mask_kl[0:SK - P] = mask.T[P:SK]
    w1 = np.concatenate([halves(L0_ffn_Ws1), L0_ffn_W1])
    w11 = np.concatenate([halves(L0_ffn_Ws11), L0_ffn_W11])
    w2 = np.concatenate([np.asarray(L0_ffn_Ws2).reshape(2, H, D), L0_ffn_W2])
    w2 = w2.reshape(NX, 2, P, D).transpose(0, 2, 1, 3).reshape(NX, P, 2 * D)
    b1 = np.concatenate([halves(L0_ffn_bs1), L0_ffn_b1]).reshape(NX * 2, P).T
    b11 = np.concatenate([halves(L0_ffn_bs11), L0_ffn_b11]).reshape(NX * 2, P).T
    arrays = {
        "x": np.asarray(x).reshape(NT, P, D).transpose(1, 0, 2),
        "ctx_t": ctx_t,
        "wq": stacked(L0_xattn_Wq),
        "wk": stacked(L0_xattn_Wk),
        "wv": np.asarray(L0_xattn_Wv).T,
        "wo": np.asarray(L0_xattn_Wo).T,
        "mask_q": mask.reshape(QT, P, SK).transpose(1, 0, 2),
        "mask_k": mask.T[0:P],
        "mask_kl": mask_kl,
        "bias_cols": np.concatenate([stacked_bias(L0_xattn_bq), stacked_bias(L0_xattn_bk), b1, b11,
                                     np.asarray(L0_ffn_bs2)[:, None]], axis=1),
        "bv_rows": np.tile(np.asarray(L0_xattn_bv), (P, 1)),
        "bo_rows": np.tile(np.asarray(L0_xattn_bo), (P, 1)),
        "wg": L0_ffn_Wg,
        "b2": L0_ffn_b2,
        "w_ffn": np.concatenate([w1, w11, w2], axis=2),
        "consts": constants(),
    }
    arrays = {name: np.ascontiguousarray(a) for name, a in arrays.items()}
    nc = bacc.Bacc("TRN2", target_bir_lowering=False, num_devices=1)
    aps = [nc.dram_tensor(name, a.shape, mybir.dt.from_np(a.dtype), kind="ExternalInput").ap()
           for name, a in arrays.items()]
    out = nc.dram_tensor("out", (P, NT, D), F32, kind="ExternalOutput").ap()
    build(nc, *aps, out)
    r = run_bass_kernel_spmd(nc, [arrays], core_ids=[0])
    return r.results[0]["out"].transpose(1, 0, 2).reshape(B, S, D)
```

```python
from contextlib import ExitStack

import concourse.bass as bass
from concourse import mybir

ALU = mybir.AluOpType
ACT = mybir.ActivationFunctionType
AX = mybir.AxisListType
F32 = mybir.dt.float32
F32R = mybir.dt.float32r
BF16 = mybir.dt.bfloat16
I32 = mybir.dt.int32
U32 = mybir.dt.uint32

P = 128
B, S, D = 4, 512, 128
NH, DK = 16, 8
SK = 154
SKP = 160
NG, HG = 4, 4
NE, H = 16, 256
NX = 18
NT = B * S // P
QT = S // P
TOK = B * S
EPS = 1e-5
MASKED = -float(2 ** 100)
BIG = 1e30
TILES = 2 * TOK // P + NE
SLOTS = TILES * P
XW = D + 2
TB = 8
NB = 3 * NE

C_ID = 0
C_MQ = 128
C_MK = 129
C_SELM = 130
C_SELO = 134
C_EPS = 138
C_DESC = 139
C_UP = 155
C_T128 = 283
C_LT = 299
C_TILE = 555
C_SPARE = C_TILE + TILES
C_DEST = C_SPARE + TILES
C_QUAD = C_DEST + 2 * NT
C_PART = C_QUAD + HG
C_EXP = C_PART + 3
C_END = C_EXP + NE
V_BQ, V_BK, V_B1, V_B11, V_BS2 = 0, 4, 8, 44, 80
V_END = 81
NPRE = 14
CW = SKP + P
BW = 2 * H + D
WE = 2 * H + 2 * D
RP = 10
LAG = 4


class Chain:

    def __init__(self, eng, sem):
        self.eng, self.sem, self.base, self.i, self.per, self.k = eng, sem, 0, 0, 0, 0

    def then(self, ins):
        self.k += 1
        ins.then_inc(self.sem, 1)
        self.eng.wait_ge(self.sem, self.i * self.per + (self.base + self.k))

    def enter(self, i, per, first):
        self.base, self.i, self.per, self.k = self.base + self.k - first * per, i, per, 0

    def leave(self, end):
        assert self.k == self.per, (self.k, self.per)
        self.base, self.i, self.per, self.k = self.base + end * self.per, 0, 0, 0


def reach(eng, sem, i, per, k):
    if isinstance(i, int) and i * per + k <= 0:
        return
    eng.wait_ge(sem, i * per + k)


def first_of(i):
    return isinstance(i, int) and i == 0


def apart(eng, passed):
    eng.sem_inc(passed, 1)


def build(nc, x, ctx_t, wq, wk, wv, wo, mask_q, mask_k, mask_kl, bias_cols, bv_rows, bo_rows, wg, b_rows,
          w_ffn, consts, out):
    stack = ExitStack()
    with stack:
        def sb(name, shape, dt=F32):
            return stack.enter_context(nc.sbuf_tensor(name, shape, dt))

        def sem(name):
            return stack.enter_context(nc.semaphore(name))

        slot_dram = nc.dram_tensor("slot_rows", (SLOTS, XW), F32, kind="Internal").ap()
        result_dram = nc.dram_tensor("result_rows", (2 * TOK + SLOTS, D), F32, kind="Internal").ap()
        cst = sb("cst", [P, C_END])
        vec = sb("vec", [P, V_END])
        xs = sb("xs", [P, NT, D])
        x_hi, x_lo = sb("x_hi", [P, TOK], F32R), sb("x_lo", [P, TOK], F32R)
        bn, mv = sb("bn", [P, NT, 6]), sb("mv", [P, NT, 2])
        std, rstd, nmr = sb("std", [P, NT]), sb("rstd", [P, NT]), sb("nmr", [P, NT])
        zero = sb("zero", [P, XW])
        wg_s, wg_hi, wg_lo = sb("wg_s", [P, NE]), sb("wg_hi", [P, NE], F32R), sb("wg_lo", [P, NE], F32R)
        w_raw = sb("w_raw", [P, 2, WE])
        up_b, one_b = sb("up_b", [P, P], BF16), sb("one_b", [P, P], BF16)
        attention = ExitStack()

        def sa(name, shape, dt=F32):
            return attention.enter_context(nc.sbuf_tensor(name, shape, dt))

        sa("weights_before", [P, NPRE, 2, WE])
        wo_s, bvr, ctx_s = sa("wo_s", [P, D]), sa("bvr", [P, D]), sa("ctx_s", [P, B, CW])
        identb, repb = sa("identb", [P, P], BF16), sa("repb", [32, HG, 32], BF16)
        mq_b, mk_b, mkl_b = sa("mq_b", [P, QT, SK], BF16), sa("mk_b", [P, S], BF16), sa("mkl_b", [32, S], BF16)
        wq_hi, wq_lo = sa("wq_hi", [P, NG * P], F32R), sa("wq_lo", [P, NG * P], F32R)
        wk_hi, wk_lo = sa("wk_hi", [P, NG * P], F32R), sa("wk_lo", [P, NG * P], F32R)
        wv_hi, wv_lo = sa("wv_hi", [P, D], F32R), sa("wv_lo", [P, D], F32R)
        mbq, mbk = sa("mbq", [P, NG]), sa("mbk", [P, NG])
        mpad = sa("mpad", [P, 2, QT, P])
        vx, vl = sa("vx", [P, NH, 32]), sa("vl", [P, NG, HG, 32])
        setup = ExitStack()

        def ss(name, shape, dt=F32):
            return setup.enter_context(nc.sbuf_tensor(name, shape, dt))

        bor = ss("bor", [P, D])
        wq_raw, wk_raw, wv_raw = ss("wq_raw", [P, NG * P]), ss("wk_raw", [P, NG * P]), ss("wv_raw", [P, D])
        mq_raw, mk_raw, mkl_raw = ss("mq_raw", [P, QT, SK], I32), ss("mk_raw", [P, S], I32), ss("mkl_raw", [32, S], I32)
        key_on = ss("key_on", [P, QT, SK])
        row_any, row_inv, row_nan = ss("row_any", [P, QT]), ss("row_inv", [P, QT]), ss("row_nan", [P, QT])
        xn = ss("xn", [P, NT, D])
        setup.close()
        c_hi, c_lo = sa("c_hi", [P, CW], F32R), sa("c_lo", [P, CW], F32R)
        k_part, k_stack = sa("k_part", [P, NG, SKP], F32R), sa("k_stack", [P, NG, SKP])
        ks, ksl = sa("ks", [P, NH, SKP], F32R), sa("ksl", [P, NG, HG, 32], F32R)
        v_all = sa("v_all", [P, 2, D])
        q_part, qs = sa("q_part", [P, 2, S], F32R), sa("qs", [P, NG, S], F32R)
        pf = sa("pf", [P, RP, S])
        o_s = sa("o_s", [P, S])
        rinv = sa("rinv", [P, QT, HG])
        on, on_t = sa("on", [P, QT, D]), sa("on_t", [P, S])
        attention.close()
        w = sb("w", [P, NX, 2, WE], F32R)
        xr = [sb(f"xr{k}", [P, NT, XW]) for k in range(2)]
        lg, top, one1, one2 = (sb(n, [P, NT, NE]) for n in ("lg", "top", "one1", "one2"))
        m1, m2, mi, g1, g2, ex = (sb(n, [P, NT]) for n in ("m1", "m2", "mi", "g1", "g2", "ex"))
        sel = sb("sel", [P, NT, NE], BF16)
        count, tiles, first_tile, end_tile = (sb(n, [P, NE]) for n in ("count", "tiles", "first_tile", "end_tile"))
        scr, scr2 = sb("scr", [P, TILES, NE]), sb("scr2", [P, NT, NE])
        slot_f, slot = sb("slot_f", [P, 2, NT]), sb("slot", [P, 2, NT], U32)
        te_f, te = sb("te_f", [1, TILES]), sb("te", [1, TILES], I32)
        first_row, end_row, from_row = sb("first_row", [NB, 1]), sb("end_row", [NB, 1]), sb("from_row", [NB, TILES])
        tile_one = sb("tile_one", [NB, TILES], BF16)
        b_raw, b_part, b_all, b_sel = (
            sb("b_raw", [NB, BW]), *(sb(n, [NB, BW], BF16) for n in ("b_part", "b_all", "b_sel")))
        shared = ExitStack()

        def sh(name, shape, dt=F32):
            return shared.enter_context(nc.sbuf_tensor(name, shape, dt))

        f_s, f_h, yt = sh("f_s", [P, 2, S]), sh("f_h", [P, 4, S]), sh("yt", [P, S])
        h_hi, h_lo = sh("h_hi", [P, 4, S], F32R), sh("h_lo", [P, 4, S], F32R)
        shared.close()
        xg = sb("xg", [P, 2, 4, XW])
        xg_hi, xg_lo = sb("xg_hi", [P, 2, 4 * P], F32R), sb("xg_lo", [P, 2, 4 * P], F32R)
        gate, dest = sb("gate", [P, TB]), sb("dest", [P, TB], U32)
        e_s, e_h = sb("e_s", [P, 2, H]), sb("e_h", [P, 2, H])
        e_hi, e_lo = sb("e_hi", [P, 2, H], F32R), sb("e_lo", [P, 2, H], F32R)
        yo = sb("yo", [P, 4, D])

        ps = stack.enter_context(nc.psum_tensor("ps", [P, 8, 512], F32))
        Q_, M_, KS_, ST_, O_, T_ = 0, 1, 2, 4, 6, 7
        CNT_, RANK_, AB_ = 2, 3, 4
        TX_, E_, TH_, Y_ = 0, 2, 4, 6

        (ld_x, ld_c, ld_w, ld_m, ld_ctx, ld_b, zeroed, dve_step, pool_passed, act_passed, dve_passed, pe_passed,
         cleared, consts_done, ln_var, ln_std, xn_done, xt_done, xhi_done, xlo_done, ctx_hi_done, ctx_split, k_mm,
         k_part_done, k_stack_done, ks_done, ksl_done, v_mm, v_done, rinv_done, vx_done, vl_done, q_mm,
         q_part_done, qs_done, smax_mm, max_done, mt_mm, qmax_done, st_mm, exp_done, pv_mm, os_done, ot_mm,
         on_done, ont_mm, ont_done, x1_mm, x1_done, w_split, b_step, lg_mm, ex_in, ex_done, copied, sel_done,
         rank_mm, slots_done, sent, tile_known, a_mm, b_mm, silu_done, h_done, hhi_done, hlo_done, w2_mm, yt_done,
         ytt_mm, x2_done, tx_mm, xghi_done, xglo_done, meta_done, e_mm, esilu_done, eh_done, th_mm, ehi_done,
         elo_done, ey_mm, yo_done, out_done, stored) = (sem(n) for n in (
            "ld_x ld_c ld_w ld_m ld_ctx ld_b zeroed dve_step pool_passed act_passed dve_passed pe_passed cleared "
            "consts_done ln_var ln_std xn_done xt_done xhi_done xlo_done ctx_hi_done ctx_split k_mm k_part_done "
            "k_stack_done ks_done ksl_done v_mm v_done rinv_done vx_done vl_done q_mm q_part_done qs_done smax_mm "
            "max_done mt_mm qmax_done st_mm exp_done pv_mm os_done ot_mm on_done ont_mm ont_done x1_mm x1_done "
            "w_split b_step lg_mm ex_in ex_done copied sel_done rank_mm slots_done sent tile_known a_mm b_mm "
            "silu_done h_done hhi_done hlo_done w2_mm yt_done ytt_mm x2_done tx_mm xghi_done xglo_done meta_done "
            "e_mm esilu_done eh_done th_mm ehi_done elo_done ey_mm yo_done out_done stored").split())
        ld_f = [sem(f"ld_f{par}") for par in range(2)]
        ld_g = [sem(f"ld_g{par}") for par in range(2)]
        ld_r = [sem(f"ld_r{c}") for c in range(B)]
        returned = [sem(f"returned{r}") for r in range(4)]
        ident = cst[:, C_ID:C_ID + P]

        block = stack.enter_context(nc.Block())

        @block.sync
        def _(sp):
            sp.dma_start(xs[:, :, :], x).then_inc(ld_x, 16)
            sp.dma_start(cst[:, :], consts).then_inc(ld_c, 16)
            sp.dma_start(vec[:, :], bias_cols).then_inc(ld_c, 16)
            for dst, src in ((wk_raw, wk), (wv_raw, wv), (wq_raw, wq), (bor, bo_rows), (wg_s, wg), (wo_s, wo),
                             (bvr, bv_rows)):
                sp.dma_start(dst[:, :], src).then_inc(ld_w, 16)
            sp.dma_start(mq_raw[:, :, :], mask_q).then_inc(ld_m, 16)
            sp.dma_start(mk_raw[:, :], mask_k).then_inc(ld_m, 16)
            sp.dma_start(mkl_raw[:, :], mask_kl).then_inc(ld_m, 16)
            sp.dma_start(ctx_s[:, :, :], ctx_t).then_inc(ld_ctx, 16)
            for e in range(2):
                sp.dma_start(w_raw[:, e, :], w_ffn[e, :, :]).then_inc(ld_f[e], 16)
            sp.wait_ge(cleared, 1)
            sp.dma_start(slot_dram.rearrange("(p s) n -> p s n", p=P),
                         zero[:, :].unsqueeze(1).to_broadcast([P, TILES, XW])).then_inc(zeroed, 16)
            with sp.Fori(1, NX // 2) as i:
                for par in range(2):
                    sp.wait_ge(w_split, i * 4 + (2 * par - 2))
                    sp.dma_start(w_raw[:, par, :],
                                 w_ffn[bass.ds(i * 2 + par, 1), :, :].rearrange("a p n -> (a p) n")).then_inc(ld_f[par], 16)
            sp.wait_ge(x1_done, B)
            sp.dma_start(b_raw[:, :], b_rows).then_inc(ld_b, 16)

            rows = slot_dram.rearrange("(g j p) n -> g p j n", p=P, j=4)
            sp.wait_ge(sent, 2 * NT * 16)
            sp.wait_ge(x2_done, B)
            for par in range(2):
                sp.dma_start(xg[:, par, :, :], rows[par]).then_inc(ld_g[par], 16)
            with sp.Fori(1, TILES // TB) as i:
                for par in range(2):
                    sp.wait_ge(tx_mm, i * 2 + (par - 1))
                    sp.wait_ge(meta_done, i * 2 + (par - 1))
                    sp.dma_start(xg[:, par, :, :], rows[bass.ds(i * 2 + par, 1), :, :, :].rearrange("g p j n -> (g p) j n")
                                 ).then_inc(ld_g[par], 16)

            for r in range(4):
                sp.wait_ge(returned[r], TILES // 4 * 16)
            for c in range(B):
                for k in range(2):
                    rows = result_dram[k * TOK + c * S:k * TOK + c * S + S, :].rearrange("(t p) d -> p t d", p=P)
                    sp.dma_start(xr[k][:, QT * c:QT * c + QT, 0:D], rows).then_inc(ld_r[c], 16)
            for c in range(B):
                sp.wait_ge(out_done, c + 1)
                sp.dma_start(out[:, QT * c:QT * c + QT, :], xs[:, QT * c:QT * c + QT, :]).then_inc(stored, 16)
            sp.wait_ge(zeroed, 16)
            sp.wait_ge(stored, 16 * B)

        @block.vector
        def _(dve):
            chain = Chain(dve, dve_step)
            link = chain.then

            def norm(src, dst, rnd):
                for t in range(NT):
                    last = dve.bn_stats(bn[:, t, :], src[:, t, :])
                link(last)
                for t in range(NT):
                    last = dve.bn_aggr(mv[:, t, :], bn[:, t, :])
                last.then_inc(ln_var, 1)
                dve.wait_ge(ln_std, rnd)
                link(dve.reciprocal(rstd[:, :], std[:, :]))
                link(dve.scalar_tensor_tensor(out=nmr[:, :], in0=mv[:, :, 0], scalar=-1.0, in1=rstd[:, :],
                                              op0=ALU.mult, op1=ALU.mult))
                for t in range(NT):
                    dve.tensor_scalar(dst[:, t, 0:D], src[:, t, :], rstd[:, t:t + 1], nmr[:, t:t + 1],
                                      ALU.mult, ALU.add).then_inc(xn_done, 1)

            def split_x(rnd):
                for c in range(4):
                    dve.wait_ge(xhi_done, 4 * (rnd - 1) + c + 1)
                    dve.tensor_tensor(x_lo[:, c * S:(c + 1) * S], ps[:, c, :],
                                      x_hi[:, c * S:(c + 1) * S].bitcast(F32), ALU.subtract).then_inc(xlo_done, 1)

            dve.memset(mpad[:, :, :, :], 0.0)
            dve.memset(vx[:, :, :], 0.0)
            dve.memset(vl[:, :, :, :], 0.0)
            dve.memset(one_b[:, :], 1.0)
            link(dve.memset(zero[:, :], 0.0))
            dve.memset(vx[:, :, DK:DK + 1], 1.0)
            for j in range(HG):
                last = dve.memset(vl[32 * j:32 * j + 32, :, j, DK:DK + 1], 1.0)
            last.then_inc(cleared, 1)
            dve.wait_ge(ld_x, 16)
            norm(xs, xn, 1)
            dve.wait_ge(ld_c, 32)
            dve.wait_ge(ld_w, 112)
            dve.tensor_copy(up_b[:, :], cst[:, C_UP:C_UP + P])
            dve.tensor_copy(identb[:, :], ident)
            dve.tensor_copy(repb[:, :, :], cst[0:32, 0:32].unsqueeze(1).to_broadcast([32, HG, 32]))
            dve.tensor_scalar(mbq[:, :], vec[:, V_BQ:V_BQ + NG], cst[:, C_MQ:C_MQ + 1], None, ALU.mult)
            dve.tensor_scalar(mbk[:, :], vec[:, V_BK:V_BK + NG], cst[:, C_MK:C_MK + 1], None, ALU.mult)
            weights = ((wk_hi, wk_lo, wk_raw), (wv_hi, wv_lo, wv_raw), (wq_hi, wq_lo, wq_raw), (wg_hi, wg_lo, wg_s))
            for hi, _, raw in weights:
                last = dve.tensor_copy(hi[:, :], raw[:, :])
            link(last)
            for hi, lo, raw in weights:
                dve.tensor_tensor(lo[:, :], raw[:, :], hi[:, :].bitcast(F32), ALU.subtract)
            dve.wait_ge(ld_m, 48)
            for dst, src in ((mq_b[:, :, :], mq_raw[:, :, :]), (mk_b[:, :], mk_raw[:, :]), (mkl_b[:, :], mkl_raw[:, :])):
                dve.tensor_scalar(dst, src, 0.0, MASKED, ALU.is_equal, ALU.mult)
            link(dve.tensor_scalar(key_on[:, :, :], mq_raw[:, :, :], 0.0, None, ALU.not_equal))
            link(dve.tensor_reduce(row_any[:, :], key_on[:, :, :], AX.X, ALU.max))
            link(dve.reciprocal(row_inv[:, :], row_any[:, :]))
            link(dve.tensor_tensor(row_nan[:, :], row_any[:, :], row_inv[:, :], ALU.mult))
            link(dve.tensor_scalar(row_nan[:, :], row_nan[:, :], -1.0, None, ALU.add))
            for q in range(QT):
                rows = xs[:, :, :].rearrange("p (b q) d -> p b q d", q=QT)[:, :, q, :]
                last = dve.scalar_tensor_tensor(out=rows, in0=rows, scalar=row_nan[:, q:q + 1],
                                                in1=bor[:, :].unsqueeze(1).to_broadcast([P, B, D]),
                                                op0=ALU.add, op1=ALU.add)
            last.then_inc(consts_done, 1)
            split_x(1)

            def key_stack(b, m):
                reach(dve, k_part_done, b, 4, m + 1)
                reach(dve, ks_done, b, 16, 4 * m + 4 - 16)
                dve.scalar_tensor_tensor(out=k_stack[:, m % 4, :], in0=ps[:, Q_, 0:SKP],
                                         scalar=vec[:, V_BK + m % 4:V_BK + m % 4 + 1], in1=k_part[:, m % 4, :].bitcast(F32),
                                         op0=ALU.add, op1=ALU.subtract).then_inc(k_stack_done, 1)

            def q_stack(b, m):
                reach(dve, q_part_done, b, 4, m + 1)
                reach(dve, st_mm, b, 20, 5 * m + 5 - 20)
                dve.scalar_tensor_tensor(out=qs[:, m % 4, :], in0=ps[:, Q_, :],
                                         scalar=vec[:, V_BQ + m % 4:V_BQ + m % 4 + 1], in1=q_part[:, m % 2, :].bitcast(F32),
                                         op0=ALU.add, op1=ALU.subtract).then_inc(qs_done, 1)

            def row_max(b, m, q):
                reach(dve, smax_mm, b, 16, 4 * m + q + 1)
                dve.tensor_reduce(mpad[:, m % 2, q, 96:96 + HG].rearrange("p (a c) -> p a c", a=2),
                                  ps[:, KS_:KS_ + 2, 0:2 * SK].rearrange("p a (c k) -> p a c k", c=2),
                                  AX.X, ALU.max, negate=True).then_inc(max_done, 1)

            def normalize(b, m):
                reach(dve, ot_mm, b, 4, m + 1)
                if m % 4 == 0:
                    reach(dve, ont_mm, b, 1, m // 4)
                o = ps[:, T_, :].rearrange("p (q j c) -> p q j c", q=QT, j=HG)
                dve.reciprocal(rinv[:, :, :], o[:, :, :, DK]).then_inc(rinv_done, 1)
                reach(dve, rinv_done, b, 4, m + 1)
                dve.tensor_tensor(on[:, :, 32 * (m % 4):32 * (m % 4) + 32].rearrange("p q (j d) -> p q j d", d=DK),
                                  o[:, :, :, 0:DK], rinv[:, :, :].unsqueeze(3).to_broadcast([P, QT, HG, DK]),
                                  ALU.mult).then_inc(on_done, 1)

            def context_low(b, nb):
                reach(dve, ctx_hi_done, b, 1, nb + 1)
                dve.tensor_tensor(c_lo[:, :], ctx_s[:, bass.ds(b + nb, 1), :].rearrange("p a n -> p (a n)"),
                                  c_hi[:, :].bitcast(F32), ALU.subtract).then_inc(ctx_split, 1)

            def value_rows(b, nb):
                reach(dve, v_mm, b, 1, nb + 1)
                reach(dve, vx_done, b, 4, 4 * nb)
                reach(dve, vl_done, b, 4, 4 * nb)
                dve.tensor_tensor(v_all[:, :, :], ps[:, M_, 0:2 * D].rearrange("p (a n) -> p a n", a=2),
                                  bvr[:, :].unsqueeze(1).to_broadcast([P, 2, D]), ALU.add).then_inc(v_done, 1)

            def add_attention(b, nb):
                reach(dve, x1_mm, b, 1, nb + 1)
                tiles = bass.ds((b + nb) * QT, QT)
                dve.tensor_tensor(xs[:, tiles, :], ps[:, T_, :].rearrange("p (q d) -> p q d", q=QT), xs[:, tiles, :],
                                  ALU.add).then_inc(x1_done, 1)

            def batch(b, last=False):
                for g in range(NG):
                    next1, next2 = not last or g + 1 < NG, not last or g + 2 < NG
                    if next1:
                        row_max(b, g + 1, 1)
                    if g == 3 and not last:
                        value_rows(b, 1)
                    if next2:
                        key_stack(b, g + 2)
                    if next1:
                        row_max(b, g + 1, 2)
                        row_max(b, g + 1, 3)
                    if g == 1 and not first_of(b):
                        add_attention(b, -1)
                    if g == 1 and not last:
                        context_low(b, 1)
                    if next2:
                        q_stack(b, g + 2)
                    if g or not first_of(b):
                        normalize(b, g - 1)
                    if next2:
                        row_max(b, g + 2, 0)

            context_low(0, 0)
            for m in range(2):
                key_stack(0, m)
                q_stack(0, m)
            value_rows(0, 0)
            for q in range(QT):
                row_max(0, 0, q)
            row_max(0, 1, 0)
            batch(0)
            with dve.Fori(1, B - 1) as b:
                batch(b)
            batch(B - 1, last=True)
            normalize(B - 1, NG - 1)
            add_attention(B - 1, 0)

            dve.wait_ge(x1_done, B)
            norm(xs, xr[0], 2)
            split_x(2)
            dve.wait_ge(lg_mm, 1)
            link(dve.tensor_copy(lg[:, :, :], ps[:, CNT_, 0:NT * NE].rearrange("p (t e) -> p t e", e=NE)))

            def row(v):
                return v[:, :].unsqueeze(2).to_broadcast([P, NT, NE])

            desc = cst[:, C_DESC:C_DESC + NE].unsqueeze(1).to_broadcast([P, NT, NE])

            def first_max(of, m, one):
                link(dve.tensor_reduce(m[:, :], of[:, :, :], AX.X, ALU.max))
                link(dve.tensor_tensor(one[:, :, :], of[:, :, :], row(m), ALU.is_equal))
                link(dve.tensor_tensor(one[:, :, :], one[:, :, :], desc, ALU.mult))
                link(dve.tensor_reduce(mi[:, :], one[:, :, :], AX.X, ALU.max))
                link(dve.tensor_tensor(one[:, :, :], row(mi), desc, ALU.is_equal))

            first_max(lg, m1, one1)
            link(dve.scalar_tensor_tensor(out=top[:, :, :], in0=one1[:, :, :], scalar=-BIG, in1=lg[:, :, :],
                                          op0=ALU.mult, op1=ALU.add))
            first_max(top, m2, one2)
            dve.tensor_tensor(m2[:, :], m2[:, :], m1[:, :], ALU.subtract).then_inc(ex_in, 1)
            dve.tensor_tensor(sel[:, :, :], one1[:, :, :], one2[:, :, :], ALU.add).then_inc(sel_done, 1)
            dve.wait_ge(ex_done, 1)
            link(dve.tensor_scalar(g2[:, :], ex[:, :], 1.0, None, ALU.add))
            link(dve.reciprocal(g1[:, :], g2[:, :]))
            dve.tensor_copy(xr[0][:, :, D:D + 1], g1[:, :].unsqueeze(2))
            dve.tensor_tensor(xr[1][:, :, D:D + 1], g1[:, :].unsqueeze(2), ex[:, :].unsqueeze(2), ALU.mult)
            dve.wait_ge(rank_mm, 1)
            link(dve.tensor_reduce(count[:, :], ps[:, CNT_, 0:NT * NE].rearrange("p (t e) -> p e t", e=NE),
                                   AX.X, ALU.add))
            full = [P, NE, NE]
            link(dve.tensor_tensor(scr[:, 0:NE, :], count[:, :].unsqueeze(2).to_broadcast(full),
                                   cst[:, C_T128:C_T128 + NE].unsqueeze(1).to_broadcast(full), ALU.is_gt))
            link(dve.tensor_reduce(tiles[:, :], scr[:, 0:NE, :], AX.X, ALU.add))
            link(dve.tensor_tensor(scr[:, 0:NE, :], tiles[:, :].unsqueeze(1).to_broadcast(full),
                                   cst[:, C_LT:C_LT + NE * NE].rearrange("p (a c) -> p a c", c=NE), ALU.mult))
            link(dve.tensor_reduce(first_tile[:, :], scr[:, 0:NE, :], AX.X, ALU.add))
            link(dve.scalar_tensor_tensor(out=top[:, :, :], in0=first_tile[:, :].unsqueeze(1).to_broadcast([P, NT, NE]),
                                          scalar=float(P),
                                          in1=ps[:, RANK_, 0:NT * NE].rearrange("p (t e) -> p t e", e=NE),
                                          op0=ALU.mult, op1=ALU.add))
            for k, one in enumerate((one1, one2)):
                link(dve.tensor_tensor(scr2[:, :, :], one[:, :, :], top[:, :, :], ALU.mult))
                link(dve.tensor_reduce(slot_f[:, k, :], scr2[:, :, :], AX.X, ALU.add))
            dve.wait_ge(copied, 1)
            for k in range(2):
                dve.tensor_tensor(xr[k][:, :, D + 1:D + 2], cst[:, C_DEST + NT * k:C_DEST + NT * k + NT].unsqueeze(2),
                                  slot_f[:, k, :].unsqueeze(2), ALU.subtract)
            dve.tensor_copy(slot[:, :, :], slot_f[:, :, :]).then_inc(slots_done, 1)
            link(dve.tensor_tensor(end_tile[:, :], first_tile[:, :], tiles[:, :], ALU.add))
            grid = [1, TILES, NE]
            link(dve.tensor_tensor(scr[0:1, :, :], cst[0:1, C_TILE:C_TILE + TILES].unsqueeze(2).to_broadcast(grid),
                                   end_tile[0:1, :].unsqueeze(1).to_broadcast(grid), ALU.is_ge))
            link(dve.tensor_reduce(te_f[:, :], scr[0:1, :, :], AX.X, ALU.add))
            dve.tensor_scalar(te[:, :], te_f[:, :], float(NE - 1), float(NX - NE), ALU.min, ALU.add)
            for of, row_ in ((first_tile, first_row), (end_tile, end_row)):
                link(dve.tensor_tensor(scr2[0:NB, 0, :], of[0:NB, :], cst[0:NB, C_EXP:C_EXP + NE], ALU.mult))
                link(dve.tensor_reduce(row_[:, :], scr2[0:NB, 0, :], AX.X, ALU.add))
            tile_row = cst[0:NB, C_TILE:C_TILE + TILES]
            link(dve.tensor_scalar(from_row[:, :], tile_row, first_row[:, 0:1], None, ALU.is_ge))
            dve.scalar_tensor_tensor(out=tile_one[:, :], in0=tile_row, scalar=end_row[:, 0:1], in1=from_row[:, :],
                                     op0=ALU.is_lt, op1=ALU.mult).then_inc(tile_known, 1)

            def linear_half(k):
                u = k % 4
                dve.wait_ge(b_mm, k + 1)
                dve.wait_ge(silu_done, k + 1)
                reach(dve, hlo_done, 0, 0, k - 3)
                dve.scalar_tensor_tensor(out=f_h[:, k % 4, :], in0=ps[:, AB_ + 2 * (k % 2) + 1, :],
                                         scalar=vec[:, V_B11 + u:V_B11 + u + 1], in1=f_s[:, k % 2, :],
                                         op0=ALU.add, op1=ALU.mult).then_inc(h_done, 1)

            def h_low(k):
                dve.wait_ge(hhi_done, k + 1)
                reach(dve, w2_mm, 0, 0, k - 3)
                dve.tensor_tensor(h_lo[:, k % 4, :], f_h[:, k % 4, :], h_hi[:, k % 4, :].bitcast(F32),
                                  ALU.subtract).then_inc(hlo_done, 1)

            def add_shared(c):
                dve.wait_ge(ytt_mm, c + 1)
                rows = xs[:, QT * c:QT * c + QT, :]
                dve.tensor_tensor(rows, ps[:, c % 2, :].rearrange("p (q d) -> p q d", q=QT), rows,
                                  ALU.add).then_inc(x2_done, 1)

            for k in range(16 + 10):
                if k < 16:
                    linear_half(k)
                if 2 <= k < 18:
                    h_low(k - 2)
                if k >= 10 and (k - 10) % 4 == 0 and (k - 10) // 4 < B:
                    add_shared((k - 10) // 4)

            def meta(i, g):
                reach(dve, ld_g[g], i, 16, 16)
                dve.tensor_copy(gate[:, 4 * g:4 * g + 4].unsqueeze(2), xg[:, g, :, D:D + 1])
                dve.tensor_tensor(dest[:, 4 * g:4 * g + 4].unsqueeze(2), xg[:, g, :, D + 1:D + 2],
                                  cst[:, bass.ds(i * TB + (C_SPARE + 4 * g), 4)].unsqueeze(2),
                                  ALU.add).then_inc(meta_done, 1)

            def x_low(i, g):
                reach(dve, xghi_done, i, 2, g + 1)
                reach(dve, e_mm, i, TB, 4 * g - 4)
                dve.tensor_tensor(xg_lo[:, g % 2, :], ps[:, TX_ + g % 2, :], xg_hi[:, g % 2, :].bitcast(F32),
                                  ALU.subtract).then_inc(xglo_done, 1)

            def hidden(i, k):
                reach(dve, esilu_done, i, TB, k + 1)
                reach(dve, th_mm, i, TB, k - 1)
                dve.tensor_tensor(e_h[:, k % 2, :], ps[:, E_ + k % 2, H:2 * H], e_s[:, k % 2, :],
                                  ALU.mult).then_inc(eh_done, 1)

            def hidden_low(i, k):
                reach(dve, ehi_done, i, TB, k + 1)
                reach(dve, ey_mm, i, TB, k - 1)
                dve.tensor_tensor(e_lo[:, k % 2, :], ps[:, TH_ + k % 2, 0:H], e_hi[:, k % 2, :].bitcast(F32),
                                  ALU.subtract).then_inc(elo_done, 1)

            def result(i, k):
                reach(dve, ey_mm, i, TB, k + 1)
                reach(dve, returned[k % 4], i, 32, 16 * (k // 4))
                reach(dve, meta_done, i, 2, k // 4 + 1)
                dve.tensor_scalar(yo[:, k % 4, :], ps[:, Y_ + k % 2, 0:D], gate[:, k % TB:k % TB + 1], None,
                                  ALU.mult).then_inc(yo_done, 1)

            def tiles_of(i, last=False):
                for k in range(TB):
                    hidden(i, k)
                    if k >= 1 or not first_of(i):
                        hidden_low(i, k - 1)
                    if k == 2:
                        x_low(i, 1)
                    if k == 6 and not last:
                        x_low(i, 2)
                    if k >= 2 or not first_of(i):
                        result(i, k - 2)
                    if k % 4 == 1:
                        meta(i, k // 4)

            x_low(0, 0)
            tiles_of(0)
            with dve.Fori(1, TILES // TB - 1) as i:
                tiles_of(i)
            i = TILES // TB - 1
            tiles_of(i, last=True)
            hidden_low(i, TB - 1)
            result(i, TB - 2)
            result(i, TB - 1)

            for c in range(B):
                dve.wait_ge(ld_r[c], 32)
                rows = xs[:, QT * c:QT * c + QT, :]
                link(dve.tensor_tensor(rows, rows, xr[0][:, QT * c:QT * c + QT, 0:D], ALU.add))
                dve.tensor_tensor(rows, rows, xr[1][:, QT * c:QT * c + QT, 0:D], ALU.add).then_inc(out_done, 1)

        @block.gpsimd
        def _(pool):
            def key_stacks(b, m):
                reach(pool, k_stack_done, b, 4, m + 1)
                reach(pool, st_mm, b, 20, 5 * m + 5 - 20)
                apart(pool, pool_passed)
                for j in range(HG):
                    pool.tensor_scalar(ks[:, HG * (m % 4) + j, :], k_stack[:, m % 4, :],
                                       cst[:, C_SELM + j:C_SELM + j + 1],
                                       cst[:, C_SELO + j:C_SELO + j + 1], ALU.mult, ALU.add).then_inc(ks_done, 1)
                reach(pool, ks_done, b, 16, 4 * m + 4)
                apart(pool, pool_passed)
                pool.tensor_copy(ksl[:, m % 4, :, :],
                                 ks[:, HG * (m % 4):HG * (m % 4) + HG, P:SKP].bitcast(F32)).then_inc(ksl_done, 1)

            def values(b, m):
                reach(pool, v_done, b, 1, m // 4 + 1)
                reach(pool, pv_mm, b, 20, 5 * m + 5 - 20)
                apart(pool, pool_passed)
                cols = slice(32 * (m % 4), 32 * (m % 4) + 32)
                pool.tensor_copy(vx[:, HG * (m % 4):HG * (m % 4) + HG, 0:DK],
                                 v_all[:, 0, cols].rearrange("p (h d) -> p h d", d=DK)).then_inc(vx_done, 1)
                pool.tensor_tensor(vl[:, m % 4, :, 0:DK],
                                   v_all[:, 1, cols].rearrange("p (j d) -> p j d", d=DK),
                                   cst[:, C_QUAD:C_QUAD + HG].unsqueeze(2).to_broadcast([P, HG, DK]),
                                   ALU.mult).then_inc(vl_done, 1)

            def split_weights(b, k):
                reach(pool, ld_f[k % 2], b, 32, 16 * (k // 2) + 16)
                apart(pool, pool_passed)
                hi, lo = (w[:, bass.ds(b * 4 + k, 1), part, :].rearrange("p a n -> p (a n)") for part in range(2))
                pool.tensor_copy(hi, w_raw[:, k % 2, :]).then_inc(w_split, 1)
                reach(pool, w_split, b, 8, 2 * k + 1)
                apart(pool, pool_passed)
                pool.tensor_tensor(lo, w_raw[:, k % 2, :], hi.bitcast(F32), ALU.subtract).then_inc(w_split, 1)

            def batch(b, last=False):
                for g in range(NG):
                    if not last or g + 2 < NG:
                        key_stacks(b, g + 2)
                    if not last or g + 1 < NG:
                        values(b, g + 1)
                    if not last:
                        split_weights(b, g + 2)

            split_weights(0, 0)
            split_weights(0, 1)
            pool.wait_ge(cleared, 1)
            pool.wait_ge(ld_c, 32)
            key_stacks(0, 0)
            key_stacks(0, 1)
            values(0, 0)
            batch(0)
            with pool.Fori(1, B - 1) as b:
                batch(b)
            batch(B - 1, last=True)

            pool.wait_ge(x1_done, B)
            for k in range(2, 6):
                split_weights(3, k)
            steps = Chain(pool, b_step)
            pool.wait_ge(ld_b, 16)
            for r in range(3):
                steps.then(pool.tensor_copy(b_part[:, :], b_raw[:, :]))
                mask = cst[0:NB, C_PART + r:C_PART + r + 1]
                if r == 0:
                    steps.then(pool.tensor_scalar(b_all[:, :], b_part[:, :], mask, None, ALU.mult))
                else:
                    steps.then(pool.tensor_scalar(b_sel[:, :], b_part[:, :], mask, None, ALU.mult))
                    steps.then(pool.tensor_tensor(b_all[:, :], b_all[:, :], b_sel[:, :], ALU.add))
                if r < 2:
                    steps.then(pool.tensor_tensor(b_raw[:, :], b_raw[:, :], b_part[:, :], ALU.subtract))

            pool.wait_ge(zeroed, 16)
            pool.wait_ge(slots_done, 1)
            for t in range(NT):
                for k in range(2):
                    pool.indirect_dma_start(out=slot_dram[:, :],
                                            out_offset=bass.IndirectOffsetOnAxis(ap=slot[:, k, t:t + 1], axis=0),
                                            in_=xr[k][:, t, :], in_offset=None).then_inc(sent, 16)

            def send(i):
                for k in range(TB):
                    reach(pool, yo_done, i, TB, k + 1)
                    apart(pool, pool_passed)
                    pool.indirect_dma_start(out=result_dram[:, :],
                                            out_offset=bass.IndirectOffsetOnAxis(ap=dest[:, k:k + 1], axis=0),
                                            in_=yo[:, k % 4, :], in_offset=None).then_inc(returned[k % 4], 16)

            send(0)
            with pool.Fori(1, TILES // TB) as i:
                send(i)

        @block.scalar
        def _(act):
            def std_dev(rnd):
                act.wait_ge(ln_var, rnd)
                act.activation(std[:, :], mv[:, :, 1], ACT.Sqrt, bias=cst[:, C_EPS:C_EPS + 1]).then_inc(ln_std, 1)

            def x_high(rnd):
                for c in range(4):
                    act.wait_ge(xt_done, 4 * (rnd - 1) + c + 1)
                    act.activation(x_hi[:, c * S:(c + 1) * S], ps[:, c, :], ACT.Copy).then_inc(xhi_done, 1)

            act.wait_ge(ld_c, 32)
            std_dev(1)
            x_high(1)
            act.wait_ge(consts_done, 1)
            act.wait_ge(ld_ctx, 16)

            def k_hi(b, m):
                reach(act, k_mm, b, 4, m + 1)
                reach(act, k_stack_done, b, 4, m + 1 - 4)
                act.activation(k_part[:, m % 4, :], ps[:, Q_, 0:SKP], ACT.Identity, bias=mbk[:, m % 4:m % 4 + 1],
                               scale=cst[:, C_MK:C_MK + 1]).then_inc(k_part_done, 1)

            def q_hi(b, m):
                reach(act, q_mm, b, 4, m + 1)
                reach(act, qs_done, b, 4, m - 1)
                act.activation(q_part[:, m % 2, :], ps[:, Q_, :], ACT.Identity, bias=mbq[:, m % 4:m % 4 + 1],
                               scale=cst[:, C_MQ:C_MQ + 1]).then_inc(q_part_done, 1)

            def q_max_rows(b, m):
                reach(act, mt_mm, b, 4, m + 1)
                act.activation(qs[96:128, m % 4, :], ps[96:128, M_, :], ACT.Copy).then_inc(qmax_done, 1)

            def exponent(b, g, t):
                n = 5 * g + t
                reach(act, st_mm, b, 20, n + 1)
                reach(act, pv_mm, b, 20, n + 1 - RP)
                act.activation(pf[:, n % RP, :], ps[:, ST_ + n % 2, :], ACT.Exp, scale=DK ** -0.5).then_inc(exp_done, 1)

            def context_high(b, nb):
                reach(act, k_mm, b, 4, 4 * nb)
                reach(act, v_mm, b, 1, nb)
                apart(act, act_passed)
                act.activation(c_hi[:, :], ctx_s[:, bass.ds(b + nb, 1), :].rearrange("p a n -> p (a n)"),
                               ACT.Copy).then_inc(ctx_hi_done, 1)

            def outputs(b, g):
                reach(act, pv_mm, b, 20, 5 * g + 5)
                reach(act, ot_mm, b, 4, g)
                act.activation(o_s[:, :], ps[:, O_, :], ACT.Copy).then_inc(os_done, 1)

            def turned_outputs(b, nb):
                reach(act, ont_mm, b, 1, nb + 1)
                reach(act, x1_mm, b, 1, nb)
                act.activation(on_t[:, :], ps[:, T_, :], ACT.Copy).then_inc(ont_done, 1)

            def batch(b, last=False):
                for g in range(NG):
                    next1, next2 = not last or g + 1 < NG, not last or g + 2 < NG
                    exponent(b, g, 0)
                    if next2:
                        k_hi(b, g + 2)
                    exponent(b, g, 1)
                    if g == 1 and not first_of(b):
                        turned_outputs(b, -1)
                    exponent(b, g, 2)
                    if g or not first_of(b):
                        outputs(b, g - 1)
                    if g == 1 and not last:
                        context_high(b, 1)
                    exponent(b, g, 3)
                    if next2:
                        q_hi(b, g + 2)
                    if next1:
                        q_max_rows(b, g + 1)
                    exponent(b, g, 4)

            context_high(0, 0)
            for m in range(2):
                k_hi(0, m)
                q_hi(0, m)
            q_max_rows(0, 0)
            batch(0)
            with act.Fori(1, B - 1) as b:
                batch(b)
            batch(B - 1, last=True)
            outputs(B - 1, NG - 1)
            turned_outputs(B - 1, 0)
            std_dev(2)
            x_high(2)
            act.activation(xr[1][:, :, 0:D], xr[0][:, :, 0:D], ACT.Copy).then_inc(copied, 1)
            act.wait_ge(ex_in, 1)
            act.activation(ex[:, :], m2[:, :], ACT.Exp).then_inc(ex_done, 1)

            def silu(k):
                u = k % 4
                act.wait_ge(a_mm, k + 1)
                reach(act, h_done, 0, 0, k - 1)
                act.activation(f_s[:, k % 2, :], ps[:, AB_ + 2 * (k % 2), :], ACT.Silu,
                               bias=vec[:, V_B1 + u:V_B1 + u + 1]).then_inc(silu_done, 1)

            def h_high(k):
                act.wait_ge(h_done, k + 1)
                reach(act, w2_mm, 0, 0, k - 3)
                act.activation(h_hi[:, k % 4, :], f_h[:, k % 4, :], ACT.Copy).then_inc(hhi_done, 1)

            def sums(c):
                act.wait_ge(w2_mm, 4 * c + 4)
                reach(act, ytt_mm, 0, 0, c)
                act.activation(yt[:, :], ps[:, c % 2, :], ACT.Identity, bias=vec[:, V_BS2:V_BS2 + 1]).then_inc(yt_done, 1)

            for k in range(16 + 8):
                if k < 16:
                    silu(k)
                if 2 <= k < 18:
                    h_high(k - 2)
                if k >= 8 and k % 4 == 0 and k // 4 - 2 < B:
                    sums(k // 4 - 2)
            act.wait_ge(x2_done, B)

            def x_group(i, g):
                reach(act, tx_mm, i, 2, g + 1)
                reach(act, e_mm, i, TB, 4 * g - 4)
                act.activation(xg_hi[:, g % 2, :], ps[:, TX_ + g % 2, :], ACT.Copy).then_inc(xghi_done, 1)

            def silu_tile(i, k):
                reach(act, e_mm, i, TB, k + 1)
                reach(act, eh_done, i, TB, k - 1)
                act.activation(e_s[:, k % 2, :], ps[:, E_ + k % 2, 0:H], ACT.Silu).then_inc(esilu_done, 1)

            def hidden_high(i, k):
                reach(act, th_mm, i, TB, k + 1)
                reach(act, ey_mm, i, TB, k - 1)
                act.activation(e_hi[:, k % 2, :], ps[:, TH_ + k % 2, 0:H], ACT.Copy).then_inc(ehi_done, 1)

            def tiles_of(i, last=False):
                for k in range(TB):
                    silu_tile(i, k)
                    if k >= 1 or not first_of(i):
                        hidden_high(i, k - 1)
                    if k == 2:
                        x_group(i, 1)
                    if k == 6 and not last:
                        x_group(i, 2)

            x_group(0, 0)
            tiles_of(0)
            with act.Fori(1, TILES // TB - 1) as i:
                tiles_of(i)
            i = TILES // TB - 1
            tiles_of(i, last=True)
            hidden_high(i, TB - 1)

        @block.tensor
        def _(pe):
            def split_mm(out_ap, w_hi_ap, w_lo_ap, m_hi_ap, m_lo_ap, start=True, stop=True):
                pe.matmul(out_ap, w_hi_ap, m_hi_ap, start=start, stop=False)
                pe.matmul(out_ap, w_hi_ap, m_lo_ap, start=False, stop=False)
                return pe.matmul(out_ap, w_lo_ap, m_hi_ap, start=False, stop=stop)

            def turn_tokens(of, rnd):
                for t in range(NT):
                    pe.wait_ge(xn_done, NT * (rnd - 1) + t + 1)
                    last = pe.transpose(ps[:, t // 4, (t % 4) * P:(t % 4 + 1) * P], of[:, t, 0:D], ident)
                    if t % 4 == 3:
                        last.then_inc(xt_done, 1)

            pe.wait_ge(ld_c, 32)
            turn_tokens(xn, 1)
            pe.wait_ge(xlo_done, 4)

            def keys(b, m):
                reach(pe, ctx_split, b, 1, m // 4 + 1)
                reach(pe, qs_done, b, 4, m)
                w = slice(P * (m % 4), P * (m % 4) + P)
                split_mm(ps[:, Q_, 0:SKP], wk_hi[:, w], wk_lo[:, w], c_hi[:, 0:SKP], c_lo[:, 0:SKP]).then_inc(k_mm, 1)

            def queries(b, m):
                reach(pe, k_stack_done, b, 4, m + 1)
                tok = bass.ds(b * S + m // 4 * S, S)
                w = slice(P * (m % 4), P * (m % 4) + P)
                split_mm(ps[:, Q_, :], wq_hi[:, w], wq_lo[:, w], x_hi[:, tok], x_lo[:, tok]).then_inc(q_mm, 1)

            def values(b, nb):
                reach(pe, qmax_done, b, 4, 4 * nb)
                for a, w in enumerate((slice(0, P), slice(SKP, SKP + P))):
                    last = split_mm(ps[:, M_, D * a:D * a + D], c_hi[:, w], c_lo[:, w], wv_hi[:, :], wv_lo[:, :])
                last.then_inc(v_mm, 1)

            def score_rows(b, m, q):
                reach(pe, qs_done, b, 4, m + 1)
                reach(pe, ks_done, b, 16, 4 * m + 4)
                reach(pe, max_done, b, 16, 4 * m + q)
                for a in range(2):
                    o = ps[:, KS_ + a, 0:2 * SK].rearrange("p (c k) -> p c k", c=2)
                    h = HG * (m % 4) + 2 * a
                    pe.matmul(o, identb[:, :], mq_b[:, q:q + 1, :].to_broadcast([P, 2, SK]), start=True, stop=False)
                    last = pe.matmul(o, qs[0:96, m % 4, P * q:P * q + P], ks[0:96, h:h + 2, 0:SK],
                                     start=False, stop=True)
                last.then_inc(smax_mm, 1)

            def turn_max(b, m):
                reach(pe, max_done, b, 16, 4 * m + 4)
                reach(pe, qmax_done, b, 4, m)
                reach(pe, v_done, b, 1, m // 4 + 1)
                for q in range(QT):
                    last = pe.transpose(ps[:, M_, P * q:P * q + P], mpad[:, m % 2, q, :], ident)
                last.then_inc(mt_mm, 1)

            def scores(b, m, t):
                n, g = 5 * m + t, m % 4
                if t == 0:
                    reach(pe, qmax_done, b, 4, m + 1)
                    reach(pe, ksl_done, b, 4, m + 1)
                reach(pe, exp_done, b, 20, n - 1)
                o = ps[:, ST_ + n % 2, :]
                if t == 0:
                    pe.matmul(o, repb[:, :, :], mkl_b[:, :], start=True, stop=False)
                    lhs = ksl[:, g, :, :]
                else:
                    pe.matmul(o, identb[:, :], mk_b[:, :], start=True, stop=False)
                    lhs = ks[:, HG * g + t - 1, 0:P]
                pe.matmul(o, lhs, qs[:, g, :], start=False, stop=True).then_inc(st_mm, 1)

            def weighted(b, m, t):
                n, g = 5 * m + t, m % 4
                if t == 0:
                    reach(pe, os_done, b, 4, m)
                    reach(pe, vx_done, b, 4, m + 1)
                    reach(pe, vl_done, b, 4, m + 1)
                    reach(pe, exp_done, b, 20, n + 5)
                    last = pe.matmul(ps[:, O_, :], vl[:, g, :, :], pf[:, n % RP, :], start=True, stop=False,
                                     skip_group_check=True)
                else:
                    j = t - 1
                    last = pe.matmul(ps[32 * j:32 * j + 32, O_, :], vx[:, HG * g + j, :], pf[:, n % RP, :],
                                     start=False, stop=True, skip_group_check=True)
                last.then_inc(pv_mm, 1)

            def turn_out(b, m):
                reach(pe, os_done, b, 4, m + 1)
                reach(pe, on_done, b, 4, m)
                if m % 4 == 0:
                    reach(pe, x1_done, b, 1, m // 4)
                for q in range(QT):
                    last = pe.transpose(ps[:, T_, P * q:P * q + P], o_s[:, P * q:P * q + P], ident)
                last.then_inc(ot_mm, 1)

            def turn_batch(b, nb):
                reach(pe, on_done, b, 4, 4 * nb + 4)
                for q in range(QT):
                    last = pe.transpose(ps[:, T_, P * q:P * q + P], on[:, q, :], ident)
                last.then_inc(ont_mm, 1)

            def project(b, nb):
                reach(pe, ont_done, b, 1, nb + 1)
                for q in range(QT):
                    last = pe.matmul(ps[:, T_, P * q:P * q + P], on_t[:, P * q:P * q + P], wo_s[:, :],
                                     start=True, stop=True)
                last.then_inc(x1_mm, 1)

            def batch(b, last=False):
                for g in range(NG):
                    next1, next2 = not last or g + 1 < NG, not last or g + 2 < NG
                    started = g or not first_of(b)
                    scores(b, g, 2)
                    if next2:
                        keys(b, g + 2)
                    if next1:
                        score_rows(b, g + 1, 1)
                    if g == 3 and not last:
                        values(b, 1)
                    if g == 1 and not first_of(b):
                        turn_batch(b, -1)
                    scores(b, g, 3)
                    if started:
                        for t in range(5):
                            weighted(b, g - 1, t)
                    if next1:
                        score_rows(b, g + 1, 2)
                    if g == 1 and not first_of(b):
                        project(b, -1)
                    scores(b, g, 4)
                    if next1:
                        score_rows(b, g + 1, 3)
                    if next2:
                        queries(b, g + 2)
                    if started:
                        turn_out(b, g - 1)
                    if next1:
                        turn_max(b, g + 1)
                        scores(b, g + 1, 0)
                        scores(b, g + 1, 1)
                    if next2:
                        score_rows(b, g + 2, 0)

            pe.wait_ge(consts_done, 1)
            for m in range(2):
                keys(0, m)
                queries(0, m)
            values(0, 0)
            for q in range(QT):
                score_rows(0, 0, q)
            turn_max(0, 0)
            score_rows(0, 1, 0)
            scores(0, 0, 0)
            scores(0, 0, 1)
            batch(0)
            with pe.Fori(1, B - 1) as b:
                batch(b)
            batch(B - 1, last=True)
            for t in range(5):
                weighted(B - 1, NG - 1, t)
            turn_out(B - 1, NG - 1)
            turn_batch(B - 1, 0)
            project(B - 1, 0)

            turn_tokens(xr[0], 2)
            pe.wait_ge(xlo_done, 8)
            for t in range(NT):
                cols = slice(P * t, P * t + P)
                last = split_mm(ps[:, CNT_, NE * t:NE * t + NE], x_hi[:, cols], x_lo[:, cols], wg_hi[:, :], wg_lo[:, :])
            last.then_inc(lg_mm, 1)

            def first(k):
                reach(pe, silu_done, 0, 0, k - 1)
                reach(pe, h_done, 0, 0, k - 1)
                e, u, tok = k % 4 // 2, k % 2, slice(k // 4 * S, k // 4 * S + S)
                for m, done in ((0, a_mm), (1, b_mm)):
                    cols = slice(H * m + P * u, H * m + P * u + P)
                    split_mm(ps[:, AB_ + 2 * (k % 2) + m, :], w[:, e, 0, cols], w[:, e, 1, cols], x_hi[:, tok],
                             x_lo[:, tok]).then_inc(done, 1)

            def second(k):
                pe.wait_ge(hlo_done, k + 1)
                c, e = k // 4, k % 4 // 2
                if k % 4 == 0:
                    reach(pe, x2_done, 0, 0, c - 1)
                cols = slice(2 * H + P * (k % 2), 2 * H + P * (k % 2) + P)
                last = split_mm(ps[:, c % 2, :], w[:, e, 0, cols], w[:, e, 1, cols], h_hi[:, k % 4, :], h_lo[:, k % 4, :],
                                start=k % 4 == 0, stop=k % 4 == 3)
                last.then_inc(w2_mm, 1)

            def turn_sums(c):
                pe.wait_ge(yt_done, c + 1)
                for q in range(QT):
                    last = pe.transpose(ps[:, c % 2, P * q:P * q + P], yt[:, P * q:P * q + P], ident)
                last.then_inc(ytt_mm, 1)

            def rank_rows():
                pe.wait_ge(sel_done, 1)
                picks = sel[:, :, :].rearrange("p t e -> p (t e)")
                pe.matmul(ps[:, CNT_, 0:NT * NE], one_b[:, :], picks, start=True, stop=True)
                pe.matmul(ps[:, RANK_, 0:NT * NE], up_b[:, :], picks, start=True, stop=True, skip_group_check=True)
                for t in range(NT - 1):
                    n = NT - 1 - t
                    last = pe.matmul(ps[:, RANK_, NE * (t + 1):NT * NE].rearrange("p (a e) -> p a e", e=NE), one_b[:, :],
                                     sel[:, t:t + 1, :].to_broadcast([P, n, NE]), start=False, stop=True,
                                     skip_group_check=True)
                last.then_inc(rank_mm, 1)

            first(0)
            first(1)
            rank_rows()
            for k in range(2, 16 + LAG + 2):
                if k < 16:
                    first(k)
                if LAG <= k < 16 + LAG:
                    second(k - LAG)
                if k >= 9 and k % 4 == 1:
                    turn_sums((k - 9) // 4)

            def expert_of(n):
                return pe.value_load(te[0:1, n:n + 1], min_val=NX - NE, max_val=NX - 1)

            def tile_biases(n, out_ap, cols):
                pe.matmul(out_ap, tile_one[:, n:n + 1].to_broadcast([NB, P]), b_all[:, cols], start=True, stop=False)

            def weights(e, part, cols):
                return w[:, bass.ds(e, 1), part, cols].rearrange("p a n -> p (a n)")

            def turn_rows(g):
                pe.wait_ge(ld_g[g % 2], 16 + 16 * (g // 2))
                reach(pe, xglo_done, 0, 0, g - 1)
                for j in range(4):
                    last = pe.transpose(ps[:, TX_ + g % 2, P * j:P * j + P], xg[:, g % 2, j, 0:D], ident)
                last.then_inc(tx_mm, 1)

            def up(n, e):
                g = n // 4
                pe.wait_ge(xglo_done, g + 1)
                reach(pe, eh_done, 0, 0, n - 1)
                o = ps[:, E_ + n % 2, :]
                tile_biases(n, o, slice(0, 2 * H))
                hi, lo = (v[:, g % 2, P * (n % 4):P * (n % 4) + P] for v in (xg_hi, xg_lo))
                split_mm(o, hi, lo, weights(e, 0, slice(0, 2 * H)), weights(e, 1, slice(0, 2 * H)),
                         start=False).then_inc(e_mm, 1)

            def turn_hidden(n):
                pe.wait_ge(eh_done, n + 1)
                reach(pe, elo_done, 0, 0, n - 1)
                for c in range(2):
                    last = pe.transpose(ps[:, TH_ + n % 2, P * c:P * c + P], e_h[:, n % 2, P * c:P * c + P], ident)
                last.then_inc(th_mm, 1)

            def down(n, e):
                pe.wait_ge(elo_done, n + 1)
                reach(pe, yo_done, 0, 0, n - 1)
                o = ps[:, Y_ + n % 2, 0:D]
                tile_biases(n, o, slice(2 * H, BW))
                for c in range(2):
                    hi, lo = (v[:, n % 2, P * c:P * c + P] for v in (e_hi, e_lo))
                    cols = slice(2 * H + D * c, 2 * H + D * c + D)
                    last = split_mm(o, hi, lo, weights(e, 0, cols), weights(e, 1, cols), start=False, stop=c == 1)
                last.then_inc(ey_mm, 1)

            pe.wait_ge(x2_done, B)
            pe.wait_ge(tile_known, 1)
            pe.wait_ge(w_split, 2 * NX)
            pe.wait_ge(b_step, 10)
            turn_rows(0)
            experts = {0: expert_of(0)}
            for n in range(TILES + 2):
                if n % 4 == 1 and n // 4 + 1 < TILES // 4:
                    turn_rows(n // 4 + 1)
                if n < TILES:
                    up(n, experts[n])
                if n + 1 < TILES:
                    experts[n + 1] = expert_of(n + 1)
                if 1 <= n <= TILES:
                    turn_hidden(n - 1)
                if n >= 2:
                    down(n - 2, experts.pop(n - 2))


def constants():
    import numpy as np
    c = np.zeros((P, C_END), np.float32)
    p = np.arange(P)
    c[:, C_ID:C_ID + P] = np.eye(P)
    c[:, C_MQ] = p // 32 == 1
    c[:, C_MK] = p // 32 == 2
    for j in range(HG):
        c[:, C_SELM + j] = (p < 96) & ((p % 32) // DK == j)
        c[:, C_SELO + j] = p == 96 + j
    c[:, C_EPS] = EPS
    for j in range(HG):
        c[:, C_QUAD + j] = p // 32 == j
    c[:, C_DESC:C_DESC + NE] = NE - np.arange(NE)
    c[:, C_UP:C_UP + P] = p[:, None] < p[None, :]
    e = np.arange(NE)
    c[:, C_T128:C_T128 + NE] = P * e
    c[:, C_LT:C_LT + NE * NE] = (e[None, :] < e[:, None]).reshape(1, -1)
    c[:, C_TILE:C_TILE + TILES] = np.arange(TILES)
    c[:, C_SPARE:C_SPARE + TILES] = 2 * TOK + P * np.arange(TILES) + p[:, None]
    for k in range(2):
        c[:, C_DEST + NT * k:C_DEST + NT * k + NT] = k * TOK + P * np.arange(NT) + p[:, None] - 2 * TOK
    for r in range(3):
        c[:, C_PART + r] = p // NE == r
    c[:, C_EXP:C_EXP + NE] = p[:, None] % NE == e
    return c


def kernel(x, ctx_1024, mask_SxS2_ik0, L0_xattn_Wq, L0_xattn_bq, L0_xattn_Wk, L0_xattn_bk, L0_xattn_Wv, L0_xattn_bv,
           L0_xattn_Wo, L0_xattn_bo, L0_ffn_Wg, L0_ffn_W1, L0_ffn_b1, L0_ffn_W11, L0_ffn_b11, L0_ffn_W2, L0_ffn_b2,
           L0_ffn_Ws1, L0_ffn_bs1, L0_ffn_Ws11, L0_ffn_bs11, L0_ffn_Ws2, L0_ffn_bs2):
    import numpy as np
    import concourse.bacc as bacc
    from concourse.bass_utils import run_bass_kernel_spmd

    def stacked(w):
        return np.tile(np.asarray(w).T.reshape(D, NG, 1, 32), (1, 1, 4, 1)).reshape(D, NG * P)

    def stacked_bias(v):
        return np.tile(np.asarray(v).reshape(NG, 1, 32), (1, 4, 1)).reshape(NG, P).T

    def halves(w):
        return np.stack([w[..., 0:H], w[..., H:2 * H]])

    ctx_t = np.zeros((D, B, CW), np.float32)
    c = np.asarray(ctx_1024).transpose(2, 0, 1)
    ctx_t[:, :, 0:SK] = c
    for j in range(HG):
        ctx_t[:, :, SKP + 32 * j:SKP + 32 * j + SK - P] = c[:, :, P:SK]
    mask = np.asarray(mask_SxS2_ik0)
    mask_kl = np.zeros((32, S), mask.dtype)
    mask_kl[0:SK - P] = mask.T[P:SK]
    w1 = np.concatenate([halves(L0_ffn_Ws1), L0_ffn_W1])
    w11 = np.concatenate([halves(L0_ffn_Ws11), L0_ffn_W11])
    w2 = np.concatenate([np.asarray(L0_ffn_Ws2).reshape(2, H, D), L0_ffn_W2])
    w2 = w2.reshape(NX, 2, P, D).transpose(0, 2, 1, 3).reshape(NX, P, 2 * D)
    b1 = np.concatenate([halves(L0_ffn_bs1), L0_ffn_b1]).reshape(NX * 2, P).T
    b11 = np.concatenate([halves(L0_ffn_bs11), L0_ffn_b11]).reshape(NX * 2, P).T
    arrays = {
        "x": np.asarray(x).reshape(NT, P, D).transpose(1, 0, 2),
        "ctx_t": ctx_t,
        "wq": stacked(L0_xattn_Wq),
        "wk": stacked(L0_xattn_Wk),
        "wv": np.asarray(L0_xattn_Wv).T,
        "wo": np.asarray(L0_xattn_Wo).T,
        "mask_q": mask.reshape(QT, P, SK).transpose(1, 0, 2),
        "mask_k": mask.T[0:P],
        "mask_kl": mask_kl,
        "bias_cols": np.concatenate([stacked_bias(L0_xattn_bq), stacked_bias(L0_xattn_bk), b1, b11,
                                     np.asarray(L0_ffn_bs2)[:, None]], axis=1),
        "bv_rows": np.tile(np.asarray(L0_xattn_bv), (P, 1)),
        "bo_rows": np.tile(np.asarray(L0_xattn_bo), (P, 1)),
        "wg": L0_ffn_Wg,
        "b_rows": np.tile(np.concatenate([L0_ffn_b1, L0_ffn_b11, L0_ffn_b2], axis=1), (3, 1)),
        "w_ffn": np.concatenate([w1, w11, w2], axis=2),
        "consts": constants(),
    }
    arrays = {name: np.ascontiguousarray(a) for name, a in arrays.items()}
    nc = bacc.Bacc("TRN2", target_bir_lowering=False, num_devices=1)
    aps = [nc.dram_tensor(name, a.shape, mybir.dt.from_np(a.dtype), kind="ExternalInput").ap()
           for name, a in arrays.items()]
    out = nc.dram_tensor("out", (P, NT, D), F32, kind="ExternalOutput").ap()
    build(nc, *aps, out)
    r = run_bass_kernel_spmd(nc, [arrays], core_ids=[0])
    return r.results[0]["out"].transpose(1, 0, 2).reshape(B, S, D)
```

```python
from contextlib import ExitStack

import concourse.bass as bass
from concourse import mybir

ALU = mybir.AluOpType
ACT = mybir.ActivationFunctionType
AX = mybir.AxisListType
F32 = mybir.dt.float32
F32R = mybir.dt.float32r
BF16 = mybir.dt.bfloat16
I32 = mybir.dt.int32
U32 = mybir.dt.uint32

P = 128
B, S, D = 4, 512, 128
NH, DK = 16, 8
SK = 154
SKP = 160
NG, HG = 4, 4
NE, H = 16, 256
NX = 18
NT = B * S // P
QT = S // P
TOK = B * S
EPS = 1e-5
MASKED = -float(2 ** 100)
BIG = 1e30
TILES = 2 * TOK // P + NE
SLOTS = TILES * P
XW = D + 2
TB = 8
NB = 3 * NE

C_ID = 0
C_MQ = 128
C_MK = 129
C_SELM = 130
C_SELO = 134
C_EPS = 138
C_DESC = 139
C_UP = 155
C_T128 = 283
C_LT = 299
C_TILE = 555
C_SPARE = C_TILE + TILES
C_DEST = C_SPARE + TILES
C_QUAD = C_DEST + 2 * NT
C_PART = C_QUAD + HG
C_EXP = C_PART + 3
C_END = C_EXP + NE
V_BQ, V_BK, V_B1, V_B11, V_BS2 = 0, 4, 8, 44, 80
V_END = 81
NPRE = 14
CW = SKP + P
BW = 2 * H + D
WE = 2 * H + 2 * D
RP = 5
LAG = 4


class Chain:

    def __init__(self, eng, sem):
        self.eng, self.sem, self.base, self.i, self.per, self.k = eng, sem, 0, 0, 0, 0

    def then(self, ins):
        self.k += 1
        ins.then_inc(self.sem, 1)
        self.eng.wait_ge(self.sem, self.i * self.per + (self.base + self.k))

    def enter(self, i, per, first):
        self.base, self.i, self.per, self.k = self.base + self.k - first * per, i, per, 0

    def leave(self, end):
        assert self.k == self.per, (self.k, self.per)
        self.base, self.i, self.per, self.k = self.base + end * self.per, 0, 0, 0


def reach(eng, sem, i, per, k):
    if isinstance(i, int) and i * per + k <= 0:
        return
    eng.wait_ge(sem, i * per + k)


def first_of(i):
    return isinstance(i, int) and i == 0


def apart(eng, passed):
    eng.sem_inc(passed, 1)


def build(nc, x, ctx_t, wq, wk, wv, wo, mask_q, mask_k, mask_kl, bias_cols, bv_rows, bo_rows, wg, b_rows,
          w_ffn, consts, out):
    stack = ExitStack()
    with stack:
        def sb(name, shape, dt=F32):
            return stack.enter_context(nc.sbuf_tensor(name, shape, dt))

        def sem(name):
            return stack.enter_context(nc.semaphore(name))

        slot_dram = nc.dram_tensor("slot_rows", (SLOTS, XW), F32, kind="Internal").ap()
        result_dram = nc.dram_tensor("result_rows", (2 * TOK + SLOTS, D), F32, kind="Internal").ap()
        cst = sb("cst", [P, C_END])
        vec = sb("vec", [P, V_END])
        xs = sb("xs", [P, NT, D])
        x_hi, x_lo = sb("x_hi", [P, TOK], F32R), sb("x_lo", [P, TOK], F32R)
        bn, mv = sb("bn", [P, NT, 6]), sb("mv", [P, NT, 2])
        std, rstd, nmr = sb("std", [P, NT]), sb("rstd", [P, NT]), sb("nmr", [P, NT])
        xr = [sb("xr0", [P, NT, XW])]
        lg = sb("lg", [P, NT, NE])
        on_t = sb("on_t", [P, S])
        xn_b, lgt = on_t[:, :].rearrange("p (q d) -> p q d", q=QT), on_t[0:NE, :]
        zero = sb("zero", [P, XW])
        wg_s, wg_hi, wg_lo = sb("wg_s", [P, NE]), sb("wg_hi", [P, NE], F32R), sb("wg_lo", [P, NE], F32R)
        w_raw = sb("w_raw", [P, 2, WE])
        up_b, one_b = sb("up_b", [P, P], BF16), sb("one_b", [P, P], BF16)
        attention = ExitStack()

        def sa(name, shape, dt=F32):
            return attention.enter_context(nc.sbuf_tensor(name, shape, dt))

        sa("weights_before", [P, NPRE, 2, WE])
        bor, row_nan = sa("bor", [P, D]), sa("row_nan", [P, QT])
        wo_s, bvr, ctx_s = sa("wo_s", [P, D]), sa("bvr", [P, D]), sa("ctx_s", [P, B, CW])
        identb, repb = sa("identb", [P, P], BF16), sa("repb", [32, HG, 32], BF16)
        mq_b, mk_b, mkl_b = sa("mq_b", [P, QT, SK], BF16), sa("mk_b", [P, S], BF16), sa("mkl_b", [32, S], BF16)
        wq_hi, wq_lo = sa("wq_hi", [P, NG * P], F32R), sa("wq_lo", [P, NG * P], F32R)
        wk_hi, wk_lo = sa("wk_hi", [P, NG * P], F32R), sa("wk_lo", [P, NG * P], F32R)
        wv_hi, wv_lo = sa("wv_hi", [P, D], F32R), sa("wv_lo", [P, D], F32R)
        mbq, mbk = sa("mbq", [P, NG]), sa("mbk", [P, NG])
        mpad = sa("mpad", [P, 2, QT, P])
        vx, vl = sa("vx", [P, NH, 32]), sa("vl", [P, NG, HG, 32])
        setup = ExitStack()

        def ss(name, shape, dt=F32):
            return setup.enter_context(nc.sbuf_tensor(name, shape, dt))

        wq_raw, wk_raw, wv_raw = ss("wq_raw", [P, NG * P]), ss("wk_raw", [P, NG * P]), ss("wv_raw", [P, D])
        mq_raw, mk_raw, mkl_raw = ss("mq_raw", [P, QT, SK], I32), ss("mk_raw", [P, S], I32), ss("mkl_raw", [32, S], I32)
        key_on = ss("key_on", [P, QT, SK])
        row_any, row_inv = ss("row_any", [P, QT]), ss("row_inv", [P, QT])
        setup.close()
        c_hi, c_lo = sa("c_hi", [P, CW], F32R), sa("c_lo", [P, CW], F32R)
        k_part, k_stack = sa("k_part", [P, 2, SKP], F32R), sa("k_stack", [P, 2, SKP])
        ks, ksl = sa("ks", [P, NH, SKP], F32R), sa("ksl", [P, NG, HG, 32], F32R)
        v_all = sa("v_all", [P, 2, D])
        q_part, qs = sa("q_part", [P, 2, S], F32R), sa("qs", [P, NG, S], F32R)
        tokens = ExitStack()
        xn = tokens.enter_context(nc.sbuf_tensor("xn", [P, NT, D], F32))
        tokens.close()
        pf = sa("pf", [P, RP, S])
        o_s = sa("o_s", [P, S])
        rinv = sa("rinv", [P, QT, HG])
        on = sa("on", [P, QT, D])
        attention.close()
        w = sb("w", [P, NX, 2, WE], F32R)
        xr.append(sb("xr1", [P, NT, XW]))
        top, one1, one2 = (sb(n, [P, NT, NE]) for n in ("top", "one1", "one2"))
        m1, m2, mi, g1, g2, ex = (sb(n, [P, NT]) for n in ("m1", "m2", "mi", "g1", "g2", "ex"))
        sel = sb("sel", [P, NT, NE], BF16)
        count, tiles, first_tile, end_tile = (sb(n, [P, NE]) for n in ("count", "tiles", "first_tile", "end_tile"))
        scr, scr2 = sb("scr", [P, NE, NE]), sb("scr2", [P, NT, NE])
        slot_f, slot = sb("slot_f", [P, 2, NT]), sb("slot", [P, 2, NT], U32)
        te_f, te = sb("te_f", [1, TILES]), sb("te", [1, TILES], I32)
        first_row, end_row, from_row = sb("first_row", [NB, 1]), sb("end_row", [NB, 1]), sb("from_row", [NB, TILES])
        tile_one = sb("tile_one", [NB, TILES], BF16)
        b_raw, b_part, b_all, b_sel = (
            sb("b_raw", [NB, BW]), *(sb(n, [NB, BW], BF16) for n in ("b_part", "b_all", "b_sel")))
        xg = sb("xg", [P, 2, 4, XW])
        yt = on_t
        shared = ExitStack()

        def sh(name, shape, dt=F32):
            return shared.enter_context(nc.sbuf_tensor(name, shape, dt))

        f_s, f_h = sh("f_s", [P, 2, S]), sh("f_h", [P, 4, S])
        h_hi, h_lo = sh("h_hi", [P, 4, S], F32R), sh("h_lo", [P, 4, S], F32R)
        shared.close()
        xg_hi, xg_lo = sb("xg_hi", [P, 2, 4 * P], F32R), sb("xg_lo", [P, 2, 4 * P], F32R)
        gate, dest = sb("gate", [P, TB]), sb("dest", [P, TB], U32)
        e_s, e_h = sb("e_s", [P, 2, H]), sb("e_h", [P, 2, H])
        e_hi, e_lo = sb("e_hi", [P, 2, H], F32R), sb("e_lo", [P, 2, H], F32R)
        half, yo = sb("half", [P, 2, D]), sb("yo", [P, 4, D])

        ps = stack.enter_context(nc.psum_tensor("ps", [P, 8, 512], F32))
        Q_, M_, KS_, ST_, O_, T_ = 0, 1, 2, 4, 6, 7
        X_ = (0, 4, 5, 6)
        CNT_, RANK_, AB_ = 2, 3, 4
        TX_, E_, TH_, Y_ = 0, 2, 4, 6

        (ld_x, ld_c, ld_w, ld_m, ld_ctx, ld_b, zeroed, dve_step, pool_passed, act_passed, dve_passed, pe_passed,
         cleared, consts_done, whi_done, ln_var, ln_std, ln_step, normed, turned_mm, turned_hi, turned_lo, lgt_mm, lgt_done,
         lgt_turned, xn_done, xt_done, xhi_done, xlo_done, ctx_hi_done, ctx_split, k_mm,
         k_part_done, k_stack_done, ks_done, ksl_done, v_mm, v_done, rinv_done, vx_done, vl_done, q_mm,
         q_part_done, qs_done, smax_mm, max_done, mt_mm, qmax_done, st_mm, exp_done, pv_mm, os_done, ot_mm,
         on_done, ont_mm, ont_done, x1_mm, x1_done, w_split, b_step, lg_done, ex_in, ex_done, copied, sel_done,
         rank_mm, slots_done, sent, tile_known, a_mm, b_mm, silu_done, h_done, hhi_done, hlo_done, w2_mm, yt_done,
         ytt_mm, x2_done, tx_mm, xghi_done, xglo_done, meta_done, e_mm, esilu_done, eh_done, th_mm, ehi_done,
         elo_done, ey_mm, half_done, yo_done, out_done, stored) = (sem(n) for n in (
            "ld_x ld_c ld_w ld_m ld_ctx ld_b zeroed dve_step pool_passed act_passed dve_passed pe_passed cleared "
            "consts_done whi_done ln_var ln_std ln_step normed turned_mm turned_hi turned_lo lgt_mm lgt_done "
            "lgt_turned xn_done xt_done xhi_done xlo_done ctx_hi_done ctx_split k_mm k_part_done "
            "k_stack_done ks_done ksl_done v_mm v_done rinv_done vx_done vl_done q_mm q_part_done qs_done smax_mm "
            "max_done mt_mm qmax_done st_mm exp_done pv_mm os_done ot_mm on_done ont_mm ont_done x1_mm x1_done "
            "w_split b_step lg_done ex_in ex_done copied sel_done rank_mm slots_done sent tile_known a_mm b_mm "
            "silu_done h_done hhi_done hlo_done w2_mm yt_done ytt_mm x2_done tx_mm xghi_done xglo_done meta_done "
            "e_mm esilu_done eh_done th_mm ehi_done elo_done ey_mm half_done yo_done out_done stored").split())
        ld_f = [sem(f"ld_f{par}") for par in range(2)]
        ld_g = [sem(f"ld_g{par}") for par in range(2)]
        ld_r = [sem(f"ld_r{c}") for c in range(B)]
        returned = [sem(f"returned{r}") for r in range(4)]
        ident = cst[:, C_ID:C_ID + P]

        block = stack.enter_context(nc.Block())

        @block.sync
        def _(sp):
            sp.dma_start(xs[:, :, :], x).then_inc(ld_x, 16)
            sp.dma_start(cst[:, :], consts).then_inc(ld_c, 16)
            sp.dma_start(vec[:, :], bias_cols).then_inc(ld_c, 16)
            for dst, src in ((wk_raw, wk), (wv_raw, wv), (wq_raw, wq), (bor, bo_rows), (wg_s, wg), (wo_s, wo),
                             (bvr, bv_rows)):
                sp.dma_start(dst[:, :], src).then_inc(ld_w, 16)
            sp.dma_start(mq_raw[:, :, :], mask_q).then_inc(ld_m, 16)
            sp.dma_start(mk_raw[:, :], mask_k).then_inc(ld_m, 16)
            sp.dma_start(mkl_raw[:, :], mask_kl).then_inc(ld_m, 16)
            sp.dma_start(ctx_s[:, :, :], ctx_t).then_inc(ld_ctx, 16)
            for e in range(2):
                sp.dma_start(w_raw[:, e, :], w_ffn[e, :, :]).then_inc(ld_f[e], 16)
            sp.wait_ge(cleared, 1)
            sp.dma_start(slot_dram.rearrange("(p s) n -> p s n", p=P),
                         zero[:, :].unsqueeze(1).to_broadcast([P, TILES, XW])).then_inc(zeroed, 16)
            with sp.Fori(1, NX // 2) as i:
                for par in range(2):
                    sp.wait_ge(w_split, i * 4 + (2 * par - 2))
                    sp.dma_start(w_raw[:, par, :],
                                 w_ffn[bass.ds(i * 2 + par, 1), :, :].rearrange("a p n -> (a p) n")).then_inc(ld_f[par], 16)
            sp.wait_ge(x1_done, B)
            sp.dma_start(b_raw[:, :], b_rows).then_inc(ld_b, 16)

            rows = slot_dram.rearrange("(g j p) n -> g p j n", p=P, j=4)
            sp.wait_ge(sent, 2 * NT * 16)
            for par in range(2):
                sp.dma_start(xg[:, par, :, :], rows[par]).then_inc(ld_g[par], 16)
            with sp.Fori(1, TILES // TB) as i:
                for par in range(2):
                    sp.wait_ge(tx_mm, i * 2 + (par - 1))
                    sp.wait_ge(meta_done, i * 2 + (par - 1))
                    sp.dma_start(xg[:, par, :, :], rows[bass.ds(i * 2 + par, 1), :, :, :].rearrange("g p j n -> (g p) j n")
                                 ).then_inc(ld_g[par], 16)

            for r in range(4):
                sp.wait_ge(returned[r], TILES // 4 * 16)
            for c in range(B):
                for k in range(2):
                    rows = result_dram[k * TOK + c * S:k * TOK + c * S + S, :].rearrange("(t p) d -> p t d", p=P)
                    sp.dma_start(xr[k][:, QT * c:QT * c + QT, 0:D], rows).then_inc(ld_r[c], 16)
            for c in range(B):
                sp.wait_ge(out_done, c + 1)
                sp.dma_start(out[:, QT * c:QT * c + QT, :], xs[:, QT * c:QT * c + QT, :]).then_inc(stored, 16)
            sp.wait_ge(zeroed, 16)
            sp.wait_ge(stored, 16 * B)

        @block.vector
        def _(dve):
            chain = Chain(dve, dve_step)
            link = chain.then

            def statistics(tiles, rows):
                for t, row in zip(tiles, rows):
                    last = dve.bn_stats(bn[:, t, :], row)
                return last

            def first_statistics():
                link(statistics(range(NT), (xs[:, t, :] for t in range(NT))))
                for t in range(NT):
                    last = dve.bn_aggr(mv[:, t, :], bn[:, t, :])
                last.then_inc(ln_var, 1)

            def first_scales():
                dve.wait_ge(ln_std, 1)
                link(dve.reciprocal(rstd[:, :], std[:, :]))
                link(dve.scalar_tensor_tensor(out=nmr[:, :], in0=mv[:, :, 0], scalar=-1.0, in1=rstd[:, :],
                                              op0=ALU.mult, op1=ALU.mult))

            def norm_block(c):
                for t in range(QT * c, QT * c + QT):
                    last = dve.tensor_scalar(xn[:, t, :], xs[:, t, :], rstd[:, t:t + 1], nmr[:, t:t + 1],
                                             ALU.mult, ALU.add)
                last.then_inc(xn_done, 1)

            def batch_rows(b, nb, q):
                return xs[:, bass.ds((b + nb) * QT + q, 1), :].rearrange("p a d -> p (a d)")

            def batch_statistics(b, nb):
                reach(dve, x1_done, b, 1, nb + 1)
                apart(dve, dve_passed)
                statistics(range(QT), (batch_rows(b, nb, q) for q in range(QT))).then_inc(ln_step, 1)
                reach(dve, ln_step, b, 3, 3 * nb + 1)
                apart(dve, dve_passed)
                for q in range(QT):
                    last = dve.bn_aggr(mv[:, q, :], bn[:, q, :])
                last.then_inc(ln_var, 1)

            def batch_norm(b, nb):
                reach(dve, ln_std, b, 1, nb + 2)
                dve.reciprocal(rstd[:, 0:QT], std[:, 0:QT]).then_inc(ln_step, 1)
                reach(dve, ln_step, b, 3, 3 * nb + 2)
                dve.scalar_tensor_tensor(out=nmr[:, 0:QT], in0=mv[:, 0:QT, 0], scalar=-1.0, in1=rstd[:, 0:QT],
                                         op0=ALU.mult, op1=ALU.mult).then_inc(ln_step, 1)
                reach(dve, ln_step, b, 3, 3 * nb + 3)
                reach(dve, turned_lo, b, 1, nb)
                for q in range(QT):
                    last = dve.tensor_scalar(xn_b[:, q, :], batch_rows(b, nb, q), rstd[:, q:q + 1], nmr[:, q:q + 1],
                                             ALU.mult, ALU.add)
                last.then_inc(normed, 1)

            def batch_low(b, nb):
                reach(dve, turned_hi, b, 1, nb + 1)
                tok = bass.ds((b + nb) * S, S)
                dve.tensor_tensor(x_lo[:, tok], ps[:, T_, :], x_hi[:, tok].bitcast(F32), ALU.subtract).then_inc(turned_lo, 1)

            def batch_logits(b, nb):
                reach(dve, lgt_turned, b, 1, nb + 1)
                dve.tensor_copy(lg[:, bass.ds((b + nb) * QT, QT), :],
                                ps[:, T_, 0:QT * NE].rearrange("p (t e) -> p t e", e=NE)).then_inc(lg_done, 1)

            def low_block(c):
                dve.wait_ge(xhi_done, c + 1)
                dve.tensor_tensor(x_lo[:, c * S:(c + 1) * S], ps[:, X_[c], :],
                                  x_hi[:, c * S:(c + 1) * S].bitcast(F32), ALU.subtract).then_inc(xlo_done, 1)

            dve.memset(mpad[:, :, :, :], 0.0)
            dve.memset(vx[:, :, :], 0.0)
            dve.memset(vl[:, :, :, :], 0.0)
            dve.memset(one_b[:, :], 1.0)
            link(dve.memset(zero[:, :], 0.0))
            dve.memset(vx[:, :, DK:DK + 1], 1.0)
            for j in range(HG):
                last = dve.memset(vl[32 * j:32 * j + 32, :, j, DK:DK + 1], 1.0)
            last.then_inc(cleared, 1)
            dve.wait_ge(ld_x, 16)
            first_statistics()
            weights = ((wk_hi, wk_lo, wk_raw), (wv_hi, wv_lo, wv_raw), (wq_hi, wq_lo, wq_raw), (wg_hi, wg_lo, wg_s))
            dve.wait_ge(whi_done, 1)
            for hi, lo, raw in weights:
                dve.tensor_tensor(lo[:, :], raw[:, :], hi[:, :].bitcast(F32), ALU.subtract)
            first_scales()
            norm_block(0)
            dve.wait_ge(ld_c, 32)
            dve.tensor_copy(up_b[:, :], cst[:, C_UP:C_UP + P])
            dve.tensor_copy(identb[:, :], ident)
            dve.tensor_copy(repb[:, :, :], cst[0:32, 0:32].unsqueeze(1).to_broadcast([32, HG, 32]))
            dve.tensor_scalar(mbq[:, :], vec[:, V_BQ:V_BQ + NG], cst[:, C_MQ:C_MQ + 1], None, ALU.mult)
            dve.tensor_scalar(mbk[:, :], vec[:, V_BK:V_BK + NG], cst[:, C_MK:C_MK + 1], None, ALU.mult)
            low_block(0)
            dve.wait_ge(ld_m, 48)
            link(dve.tensor_scalar(key_on[:, :, :], mq_raw[:, :, :], 0.0, None, ALU.not_equal))
            link(dve.tensor_reduce(row_any[:, :], key_on[:, :, :], AX.X, ALU.max))
            link(dve.reciprocal(row_inv[:, :], row_any[:, :]))
            link(dve.tensor_tensor(row_nan[:, :], row_any[:, :], row_inv[:, :], ALU.mult))
            link(dve.tensor_scalar(row_nan[:, :], row_nan[:, :], -1.0, None, ALU.add))
            for dst, src in ((mq_b[:, :, :], mq_raw[:, :, :]), (mk_b[:, :], mk_raw[:, :]), (mkl_b[:, :], mkl_raw[:, :])):
                last = dve.tensor_scalar(dst, src, 0.0, MASKED, ALU.is_equal, ALU.mult)
            last.then_inc(consts_done, 1)
            norm_block(1)

            def add_bias(q):
                rows = xs[:, :, :].rearrange("p (b q) d -> p b q d", q=QT)[:, :, q, :]
                return dve.scalar_tensor_tensor(out=rows, in0=rows, scalar=row_nan[:, q:q + 1],
                                                in1=bor[:, :].unsqueeze(1).to_broadcast([P, B, D]),
                                                op0=ALU.add, op1=ALU.add)

            def key_stack(b, m):
                reach(dve, k_part_done, b, 4, m + 1)
                reach(dve, ks_done, b, 16, 4 * m - 4)
                dve.scalar_tensor_tensor(out=k_stack[:, m % 2, :], in0=ps[:, Q_, 0:SKP],
                                         scalar=vec[:, V_BK + m % 4:V_BK + m % 4 + 1], in1=k_part[:, m % 2, :].bitcast(F32),
                                         op0=ALU.add, op1=ALU.subtract).then_inc(k_stack_done, 1)

            def q_stack(b, m):
                reach(dve, q_part_done, b, 4, m + 1)
                reach(dve, st_mm, b, 20, 5 * m + 5 - 20)
                dve.scalar_tensor_tensor(out=qs[:, m % 4, :], in0=ps[:, Q_, :],
                                         scalar=vec[:, V_BQ + m % 4:V_BQ + m % 4 + 1], in1=q_part[:, m % 2, :].bitcast(F32),
                                         op0=ALU.add, op1=ALU.subtract).then_inc(qs_done, 1)

            def row_max(b, m, q):
                for a in range(2):
                    reach(dve, smax_mm, b, 32, 8 * m + 2 * q + a + 1)
                    dve.tensor_reduce(mpad[:, m % 2, q, 96 + 2 * a:98 + 2 * a],
                                      ps[:, KS_ + a, 0:2 * SK].rearrange("p (c k) -> p c k", c=2),
                                      AX.X, ALU.max, negate=True).then_inc(max_done, 1)

            def normalize(b, m):
                reach(dve, ot_mm, b, 4, m + 1)
                if m % 4 == 0:
                    reach(dve, ont_mm, b, 1, m // 4)
                o = ps[:, T_, :].rearrange("p (q j c) -> p q j c", q=QT, j=HG)
                dve.reciprocal(rinv[:, :, :], o[:, :, :, DK]).then_inc(rinv_done, 1)
                reach(dve, rinv_done, b, 4, m + 1)
                dve.tensor_tensor(on[:, :, 32 * (m % 4):32 * (m % 4) + 32].rearrange("p q (j d) -> p q j d", d=DK),
                                  o[:, :, :, 0:DK], rinv[:, :, :].unsqueeze(3).to_broadcast([P, QT, HG, DK]),
                                  ALU.mult).then_inc(on_done, 1)

            def context_low(b, nb):
                reach(dve, ctx_hi_done, b, 1, nb + 1)
                dve.tensor_tensor(c_lo[:, :], ctx_s[:, bass.ds(b + nb, 1), :].rearrange("p a n -> p (a n)"),
                                  c_hi[:, :].bitcast(F32), ALU.subtract).then_inc(ctx_split, 1)

            def value_rows(b, nb):
                reach(dve, v_mm, b, 1, nb + 1)
                reach(dve, vx_done, b, 4, 4 * nb)
                reach(dve, vl_done, b, 4, 4 * nb)
                dve.tensor_tensor(v_all[:, :, :], ps[:, M_, 0:2 * D].rearrange("p (a n) -> p a n", a=2),
                                  bvr[:, :].unsqueeze(1).to_broadcast([P, 2, D]), ALU.add).then_inc(v_done, 1)

            def add_attention(b, nb):
                reach(dve, x1_mm, b, 1, nb + 1)
                tiles = bass.ds((b + nb) * QT, QT)
                dve.tensor_tensor(xs[:, tiles, :], ps[:, T_, :].rearrange("p (q d) -> p q d", q=QT), xs[:, tiles, :],
                                  ALU.add).then_inc(x1_done, 1)

            def batch(b, last=False):
                for g in range(NG):
                    next1, next2 = not last or g + 1 < NG, not last or g + 2 < NG
                    if next1:
                        row_max(b, g + 1, 1)
                    if g == 3 and not last:
                        value_rows(b, 1)
                    if next2:
                        key_stack(b, g + 2)
                    if next1:
                        row_max(b, g + 1, 2)
                    if g == 3 and not first_of(b):
                        batch_logits(b, -1)
                    if next1:
                        row_max(b, g + 1, 3)
                    if g == 1 and not first_of(b):
                        add_attention(b, -1)
                        batch_statistics(b, -1)
                    if g == 2 and not first_of(b):
                        batch_low(b, -1)
                    if g == 1 and not last:
                        context_low(b, 1)
                    if next2:
                        q_stack(b, g + 2)
                    if g or not first_of(b):
                        normalize(b, g - 1)
                    if next2:
                        row_max(b, g + 2, 0)
                    if g == 1 and not first_of(b):
                        batch_norm(b, -1)

            context_low(0, 0)
            norm_block(2)
            key_stack(0, 0)
            norm_block(3)
            q_stack(0, 0)
            low_block(1)
            row_max(0, 0, 0)
            key_stack(0, 1)
            row_max(0, 0, 1)
            low_block(2)
            row_max(0, 0, 2)
            q_stack(0, 1)
            row_max(0, 0, 3)
            value_rows(0, 0)
            low_block(3)
            for q in range(QT):
                last = add_bias(q)
            link(last)
            row_max(0, 1, 0)
            batch(0)
            with dve.Fori(1, B - 1) as b:
                batch(b)
            batch(B - 1, last=True)
            normalize(B - 1, NG - 1)
            add_attention(B - 1, 0)

            batch_statistics(B - 1, 0)
            batch_norm(B - 1, 0)
            batch_low(B - 1, 0)
            batch_logits(B - 1, 0)
            dve.wait_ge(lg_done, B)

            def row(v):
                return v[:, :].unsqueeze(2).to_broadcast([P, NT, NE])

            desc = cst[:, C_DESC:C_DESC + NE].unsqueeze(1).to_broadcast([P, NT, NE])

            def first_max(of, m, one):
                link(dve.tensor_reduce(m[:, :], of[:, :, :], AX.X, ALU.max))
                link(dve.tensor_tensor(one[:, :, :], of[:, :, :], row(m), ALU.is_equal))
                link(dve.tensor_tensor(one[:, :, :], one[:, :, :], desc, ALU.mult))
                link(dve.tensor_reduce(mi[:, :], one[:, :, :], AX.X, ALU.max))
                link(dve.tensor_tensor(one[:, :, :], row(mi), desc, ALU.is_equal))

            first_max(lg, m1, one1)
            link(dve.scalar_tensor_tensor(out=top[:, :, :], in0=one1[:, :, :], scalar=-BIG, in1=lg[:, :, :],
                                          op0=ALU.mult, op1=ALU.add))
            first_max(top, m2, one2)
            dve.tensor_tensor(m2[:, :], m2[:, :], m1[:, :], ALU.subtract).then_inc(ex_in, 1)
            dve.tensor_tensor(sel[:, :, :], one1[:, :, :], one2[:, :, :], ALU.add).then_inc(sel_done, 1)
            dve.wait_ge(ex_done, 1)
            link(dve.tensor_scalar(g2[:, :], ex[:, :], 1.0, None, ALU.add))
            link(dve.reciprocal(g1[:, :], g2[:, :]))
            dve.tensor_copy(xr[0][:, :, D:D + 1], g1[:, :].unsqueeze(2))
            dve.tensor_tensor(xr[1][:, :, D:D + 1], g1[:, :].unsqueeze(2), ex[:, :].unsqueeze(2), ALU.mult)
            dve.wait_ge(rank_mm, 1)
            link(dve.tensor_reduce(count[:, :], ps[:, CNT_, 0:NT * NE].rearrange("p (t e) -> p e t", e=NE),
                                   AX.X, ALU.add))
            full = [P, NE, NE]
            link(dve.tensor_tensor(scr[:, :, :], count[:, :].unsqueeze(2).to_broadcast(full),
                                   cst[:, C_T128:C_T128 + NE].unsqueeze(1).to_broadcast(full), ALU.is_gt))
            link(dve.tensor_reduce(tiles[:, :], scr[:, :, :], AX.X, ALU.add))
            link(dve.tensor_tensor(scr[:, :, :], tiles[:, :].unsqueeze(1).to_broadcast(full),
                                   cst[:, C_LT:C_LT + NE * NE].rearrange("p (a c) -> p a c", c=NE), ALU.mult))
            link(dve.tensor_reduce(first_tile[:, :], scr[:, :, :], AX.X, ALU.add))
            link(dve.scalar_tensor_tensor(out=top[:, :, :], in0=first_tile[:, :].unsqueeze(1).to_broadcast([P, NT, NE]),
                                          scalar=float(P),
                                          in1=ps[:, RANK_, 0:NT * NE].rearrange("p (t e) -> p t e", e=NE),
                                          op0=ALU.mult, op1=ALU.add))
            for k, one in enumerate((one1, one2)):
                link(dve.tensor_tensor(scr2[:, :, :], one[:, :, :], top[:, :, :], ALU.mult))
                link(dve.tensor_reduce(slot_f[:, k, :], scr2[:, :, :], AX.X, ALU.add))
            dve.wait_ge(copied, 1)
            for k in range(2):
                dve.tensor_tensor(xr[k][:, :, D + 1:D + 2], cst[:, C_DEST + NT * k:C_DEST + NT * k + NT].unsqueeze(2),
                                  slot_f[:, k, :].unsqueeze(2), ALU.subtract)
            dve.tensor_copy(slot[:, :, :], slot_f[:, :, :]).then_inc(slots_done, 1)
            def linear_half(k):
                u = k % 4
                dve.wait_ge(b_mm, k + 1)
                dve.wait_ge(silu_done, k + 1)
                reach(dve, hlo_done, 0, 0, k - 3)
                dve.scalar_tensor_tensor(out=f_h[:, k % 4, :], in0=ps[:, AB_ + 2 * (k % 2) + 1, :],
                                         scalar=vec[:, V_B11 + u:V_B11 + u + 1], in1=f_s[:, k % 2, :],
                                         op0=ALU.add, op1=ALU.mult).then_inc(h_done, 1)

            def h_low(k):
                dve.wait_ge(hhi_done, k + 1)
                reach(dve, w2_mm, 0, 0, k - 3)
                dve.tensor_tensor(h_lo[:, k % 4, :], f_h[:, k % 4, :], h_hi[:, k % 4, :].bitcast(F32),
                                  ALU.subtract).then_inc(hlo_done, 1)

            def add_shared(c):
                dve.wait_ge(ytt_mm, c + 1)
                rows = xs[:, QT * c:QT * c + QT, :]
                dve.tensor_tensor(rows, ps[:, c % 2, :].rearrange("p (q d) -> p q d", q=QT), rows,
                                  ALU.add).then_inc(x2_done, 1)

            def bias_step(k):
                reach(dve, b_step, 0, 0, k)
                mask = cst[0:NB, C_PART + (0, 0, 0, 1, 1, 1, 1, 2, 2, 2)[k]:][:, 0:1]
                if k in (0, 3, 7):
                    ins = dve.tensor_copy(b_part[:, :], b_raw[:, :])
                elif k == 1:
                    ins = dve.tensor_scalar(b_all[:, :], b_part[:, :], mask, None, ALU.mult)
                elif k in (4, 8):
                    ins = dve.tensor_scalar(b_sel[:, :], b_part[:, :], mask, None, ALU.mult)
                elif k in (5, 9):
                    ins = dve.tensor_tensor(b_all[:, :], b_all[:, :], b_sel[:, :], ALU.add)
                else:
                    ins = dve.tensor_tensor(b_raw[:, :], b_raw[:, :], b_part[:, :], ALU.subtract)
                ins.then_inc(b_step, 1)

            def tile_experts():
                link(dve.tensor_tensor(end_tile[:, :], first_tile[:, :], tiles[:, :], ALU.add))
                grid = [1, NE, NE]
                for c in range(0, TILES, NE):
                    link(dve.tensor_tensor(scr[0:1, :, :], cst[0:1, C_TILE + c:C_TILE + c + NE].unsqueeze(2).to_broadcast(grid),
                                           end_tile[0:1, :].unsqueeze(1).to_broadcast(grid), ALU.is_ge))
                    link(dve.tensor_reduce(te_f[:, c:c + NE], scr[0:1, :, :], AX.X, ALU.add))
                dve.tensor_scalar(te[:, :], te_f[:, :], float(NE - 1), float(NX - NE), ALU.min, ALU.add)
                for of, row_ in ((first_tile, first_row), (end_tile, end_row)):
                    link(dve.tensor_tensor(scr2[0:NB, 0, :], of[0:NB, :], cst[0:NB, C_EXP:C_EXP + NE], ALU.mult))
                    link(dve.tensor_reduce(row_[:, :], scr2[0:NB, 0, :], AX.X, ALU.add))
                tile_row = cst[0:NB, C_TILE:C_TILE + TILES]
                link(dve.tensor_scalar(from_row[:, :], tile_row, first_row[:, 0:1], None, ALU.is_ge))
                dve.scalar_tensor_tensor(out=tile_one[:, :], in0=tile_row, scalar=end_row[:, 0:1], in1=from_row[:, :],
                                         op0=ALU.is_lt, op1=ALU.mult).then_inc(tile_known, 1)

            dve.wait_ge(ld_b, 16)
            for k in range(16 + 10):
                if k < 16:
                    linear_half(k)
                if k < 10:
                    bias_step(k)
                if k == 12:
                    tile_experts()
                if 2 <= k < 18:
                    h_low(k - 2)
                if k >= 10 and (k - 10) % 4 == 0 and (k - 10) // 4 < B:
                    add_shared((k - 10) // 4)

            def meta(i, g):
                reach(dve, ld_g[g], i, 16, 16)
                dve.tensor_copy(gate[:, 4 * g:4 * g + 4].unsqueeze(2), xg[:, g, :, D:D + 1])
                dve.tensor_tensor(dest[:, 4 * g:4 * g + 4].unsqueeze(2), xg[:, g, :, D + 1:D + 2],
                                  cst[:, bass.ds(i * TB + (C_SPARE + 4 * g), 4)].unsqueeze(2),
                                  ALU.add).then_inc(meta_done, 1)

            def x_low(i, g):
                reach(dve, xghi_done, i, 2, g + 1)
                reach(dve, e_mm, i, TB, 4 * g - 4)
                dve.tensor_tensor(xg_lo[:, g % 2, :], ps[:, TX_ + g % 2, :], xg_hi[:, g % 2, :].bitcast(F32),
                                  ALU.subtract).then_inc(xglo_done, 1)

            def hidden(i, k):
                reach(dve, esilu_done, i, TB, k + 1)
                reach(dve, th_mm, i, TB, k - 1)
                dve.tensor_tensor(e_h[:, k % 2, :], ps[:, E_ + k % 2, H:2 * H], e_s[:, k % 2, :],
                                  ALU.mult).then_inc(eh_done, 1)

            def hidden_low(i, k):
                reach(dve, ehi_done, i, TB, k + 1)
                reach(dve, ey_mm, i, TB, k - 1)
                dve.tensor_tensor(e_lo[:, k % 2, :], ps[:, TH_ + k % 2, 0:H], e_hi[:, k % 2, :].bitcast(F32),
                                  ALU.subtract).then_inc(elo_done, 1)

            def result_half(i, k):
                reach(dve, ey_mm, i, TB, k + 1)
                reach(dve, meta_done, i, 2, k // 4 + 1)
                dve.tensor_scalar(half[:, k % 2, :], ps[:, Y_ + k % 2, D:2 * D], gate[:, k % TB:k % TB + 1], None,
                                  ALU.mult).then_inc(half_done, 1)

            def result(i, k):
                reach(dve, half_done, i, TB, k + 1)
                reach(dve, returned[k % 4], i, 32, 16 * (k // 4))
                dve.scalar_tensor_tensor(out=yo[:, k % 4, :], in0=ps[:, Y_ + k % 2, 0:D], scalar=gate[:, k % TB:k % TB + 1],
                                         in1=half[:, k % 2, :], op0=ALU.mult, op1=ALU.add).then_inc(yo_done, 1)

            def tiles_of(i, last=False):
                for k in range(TB):
                    hidden(i, k)
                    if k >= 2 or not first_of(i):
                        result_half(i, k - 2)
                    if k >= 1 or not first_of(i):
                        hidden_low(i, k - 1)
                    if k == 2:
                        x_low(i, 1)
                    if k == 6 and not last:
                        x_low(i, 2)
                    if k >= 2 or not first_of(i):
                        result(i, k - 2)
                    if k % 4 == 1:
                        meta(i, k // 4)

            x_low(0, 0)
            tiles_of(0)
            with dve.Fori(1, TILES // TB - 1) as i:
                tiles_of(i)
            i = TILES // TB - 1
            tiles_of(i, last=True)
            hidden_low(i, TB - 1)
            for k in (TB - 2, TB - 1):
                result_half(i, k)
                result(i, k)

            for c in range(B):
                dve.wait_ge(ld_r[c], 32)
                rows = xs[:, QT * c:QT * c + QT, :]
                link(dve.tensor_tensor(rows, rows, xr[0][:, QT * c:QT * c + QT, 0:D], ALU.add))
                dve.tensor_tensor(rows, rows, xr[1][:, QT * c:QT * c + QT, 0:D], ALU.add).then_inc(out_done, 1)

        @block.gpsimd
        def _(pool):
            def key_stacks(b, m):
                reach(pool, k_stack_done, b, 4, m + 1)
                reach(pool, st_mm, b, 20, 5 * m + 5 - 20)
                apart(pool, pool_passed)
                for j in range(HG):
                    pool.tensor_scalar(ks[:, HG * (m % 4) + j, :], k_stack[:, m % 2, :],
                                       cst[:, C_SELM + j:C_SELM + j + 1],
                                       cst[:, C_SELO + j:C_SELO + j + 1], ALU.mult, ALU.add).then_inc(ks_done, 1)
                reach(pool, ks_done, b, 16, 4 * m + 4)
                apart(pool, pool_passed)
                pool.tensor_copy(ksl[:, m % 4, :, :],
                                 ks[:, HG * (m % 4):HG * (m % 4) + HG, P:SKP].bitcast(F32)).then_inc(ksl_done, 1)

            def values(b, m):
                reach(pool, v_done, b, 1, m // 4 + 1)
                reach(pool, pv_mm, b, 20, 5 * m + 5 - 20)
                apart(pool, pool_passed)
                cols = slice(32 * (m % 4), 32 * (m % 4) + 32)
                pool.tensor_copy(vx[:, HG * (m % 4):HG * (m % 4) + HG, 0:DK],
                                 v_all[:, 0, cols].rearrange("p (h d) -> p h d", d=DK)).then_inc(vx_done, 1)
                pool.tensor_tensor(vl[:, m % 4, :, 0:DK],
                                   v_all[:, 1, cols].rearrange("p (j d) -> p j d", d=DK),
                                   cst[:, C_QUAD:C_QUAD + HG].unsqueeze(2).to_broadcast([P, HG, DK]),
                                   ALU.mult).then_inc(vl_done, 1)

            def split_weights(b, k):
                reach(pool, ld_f[k % 2], b, 32, 16 * (k // 2) + 16)
                apart(pool, pool_passed)
                hi, lo = (w[:, bass.ds(b * 4 + k, 1), part, :].rearrange("p a n -> p (a n)") for part in range(2))
                pool.tensor_copy(hi, w_raw[:, k % 2, :]).then_inc(w_split, 1)
                reach(pool, w_split, b, 8, 2 * k + 1)
                apart(pool, pool_passed)
                pool.tensor_tensor(lo, w_raw[:, k % 2, :], hi.bitcast(F32), ALU.subtract).then_inc(w_split, 1)

            def batch(b, last=False):
                for g in range(NG):
                    if not last or g + 2 < NG:
                        key_stacks(b, g + 2)
                    if not last or g + 1 < NG:
                        values(b, g + 1)
                    if not last:
                        split_weights(b, g + 2)

            split_weights(0, 0)
            split_weights(0, 1)
            pool.wait_ge(cleared, 1)
            pool.wait_ge(ld_c, 32)
            key_stacks(0, 0)
            key_stacks(0, 1)
            values(0, 0)
            batch(0)
            with pool.Fori(1, B - 1) as b:
                batch(b)
            batch(B - 1, last=True)

            pool.wait_ge(x1_done, B)
            for k in range(2, 6):
                split_weights(3, k)

            pool.wait_ge(zeroed, 16)
            pool.wait_ge(slots_done, 1)
            for t in range(NT):
                for k in range(2):
                    pool.indirect_dma_start(out=slot_dram[:, :],
                                            out_offset=bass.IndirectOffsetOnAxis(ap=slot[:, k, t:t + 1], axis=0),
                                            in_=xr[k][:, t, :], in_offset=None).then_inc(sent, 16)

            def send(i):
                for k in range(TB):
                    reach(pool, yo_done, i, TB, k + 1)
                    apart(pool, pool_passed)
                    pool.indirect_dma_start(out=result_dram[:, :],
                                            out_offset=bass.IndirectOffsetOnAxis(ap=dest[:, k:k + 1], axis=0),
                                            in_=yo[:, k % 4, :], in_offset=None).then_inc(returned[k % 4], 16)

            send(0)
            with pool.Fori(1, TILES // TB) as i:
                send(i)

        @block.scalar
        def _(act):
            def std_dev(n):
                act.activation(std[:, 0:n], mv[:, 0:n, 1], ACT.Sqrt, bias=cst[:, C_EPS:C_EPS + 1]).then_inc(ln_std, 1)

            def batch_std(b, nb):
                reach(act, ln_var, b, 1, nb + 2)
                std_dev(QT)

            def batch_high(b, nb):
                reach(act, turned_mm, b, 1, nb + 1)
                apart(act, act_passed)
                act.activation(x_hi[:, bass.ds((b + nb) * S, S)], ps[:, T_, :], ACT.Copy)
                act.activation(xr[0][:, bass.ds((b + nb) * QT, QT), 0:D], xn_b[:, :, :], ACT.Copy).then_inc(turned_hi, 1)

            def batch_logits(b, nb):
                reach(act, lgt_mm, b, 1, nb + 1)
                act.activation(lgt[:, :], ps[0:NE, T_, :], ACT.Copy).then_inc(lgt_done, 1)

            def high_block(c):
                act.wait_ge(xt_done, c + 1)
                act.activation(x_hi[:, c * S:(c + 1) * S], ps[:, X_[c], :], ACT.Copy).then_inc(xhi_done, 1)

            act.wait_ge(ld_w, 112)
            for hi, raw in ((wk_hi, wk_raw), (wv_hi, wv_raw), (wq_hi, wq_raw), (wg_hi, wg_s)):
                last = act.activation(hi[:, :], raw[:, :], ACT.Copy)
            last.then_inc(whi_done, 1)
            act.wait_ge(ld_c, 32)
            act.wait_ge(ln_var, 1)
            std_dev(NT)
            high_block(0)
            act.wait_ge(consts_done, 1)
            act.wait_ge(ld_ctx, 16)

            def k_hi(b, m):
                reach(act, k_mm, b, 4, m + 1)
                reach(act, k_stack_done, b, 4, m - 1)
                act.activation(k_part[:, m % 2, :], ps[:, Q_, 0:SKP], ACT.Identity, bias=mbk[:, m % 4:m % 4 + 1],
                               scale=cst[:, C_MK:C_MK + 1]).then_inc(k_part_done, 1)

            def q_hi(b, m):
                reach(act, q_mm, b, 4, m + 1)
                reach(act, qs_done, b, 4, m - 1)
                act.activation(q_part[:, m % 2, :], ps[:, Q_, :], ACT.Identity, bias=mbq[:, m % 4:m % 4 + 1],
                               scale=cst[:, C_MQ:C_MQ + 1]).then_inc(q_part_done, 1)

            def q_max_rows(b, m):
                reach(act, mt_mm, b, 4, m + 1)
                act.activation(qs[96:128, m % 4, :], ps[96:128, M_, :], ACT.Copy).then_inc(qmax_done, 1)

            def exponent(b, g, t):
                n = 5 * g + t
                reach(act, st_mm, b, 20, n + 1)
                reach(act, pv_mm, b, 20, n + 1 - RP)
                act.activation(pf[:, n % RP, :], ps[:, ST_ + n % 2, :], ACT.Exp, scale=DK ** -0.5).then_inc(exp_done, 1)

            def context_high(b, nb):
                reach(act, k_mm, b, 4, 4 * nb)
                reach(act, v_mm, b, 1, nb)
                apart(act, act_passed)
                act.activation(c_hi[:, :], ctx_s[:, bass.ds(b + nb, 1), :].rearrange("p a n -> p (a n)"),
                               ACT.Copy).then_inc(ctx_hi_done, 1)

            def outputs(b, g):
                reach(act, pv_mm, b, 20, 5 * g + 5)
                reach(act, ot_mm, b, 4, g)
                act.activation(o_s[:, :], ps[:, O_, :], ACT.Copy).then_inc(os_done, 1)

            def turned_outputs(b, nb):
                reach(act, ont_mm, b, 1, nb + 1)
                reach(act, x1_mm, b, 1, nb)
                act.activation(on_t[:, :], ps[:, T_, :], ACT.Copy).then_inc(ont_done, 1)

            def batch(b, last=False):
                for g in range(NG):
                    next1, next2 = not last or g + 1 < NG, not last or g + 2 < NG
                    exponent(b, g, 0)
                    exponent(b, g, 1)
                    if next2:
                        k_hi(b, g + 2)
                    if g or not first_of(b):
                        outputs(b, g - 1)
                    if g == 1 and not first_of(b):
                        turned_outputs(b, -1)
                    exponent(b, g, 2)
                    if g == 1 and not last:
                        context_high(b, 1)
                    exponent(b, g, 3)
                    if g == 2 and not first_of(b):
                        batch_high(b, -1)
                    if g == 3 and not first_of(b):
                        batch_logits(b, -1)
                    if next2:
                        q_hi(b, g + 2)
                    if next1:
                        q_max_rows(b, g + 1)
                    exponent(b, g, 4)
                    if g == 1 and not first_of(b):
                        batch_std(b, -1)

            context_high(0, 0)
            high_block(1)
            k_hi(0, 0)
            high_block(2)
            q_hi(0, 0)
            high_block(3)
            k_hi(0, 1)
            q_hi(0, 1)
            q_max_rows(0, 0)
            batch(0)
            with act.Fori(1, B - 1) as b:
                batch(b)
            batch(B - 1, last=True)
            outputs(B - 1, NG - 1)
            turned_outputs(B - 1, 0)
            batch_std(B - 1, 0)
            batch_high(B - 1, 0)
            batch_logits(B - 1, 0)
            act.activation(xr[1][:, :, 0:D], xr[0][:, :, 0:D], ACT.Copy).then_inc(copied, 1)
            act.wait_ge(ex_in, 1)
            act.activation(ex[:, :], m2[:, :], ACT.Exp).then_inc(ex_done, 1)

            def silu(k):
                u = k % 4
                act.wait_ge(a_mm, k + 1)
                reach(act, h_done, 0, 0, k - 1)
                act.activation(f_s[:, k % 2, :], ps[:, AB_ + 2 * (k % 2), :], ACT.Silu,
                               bias=vec[:, V_B1 + u:V_B1 + u + 1]).then_inc(silu_done, 1)

            def h_high(k):
                act.wait_ge(h_done, k + 1)
                reach(act, w2_mm, 0, 0, k - 3)
                act.activation(h_hi[:, k % 4, :], f_h[:, k % 4, :], ACT.Copy).then_inc(hhi_done, 1)

            def sums(c):
                act.wait_ge(w2_mm, 4 * c + 4)
                reach(act, ytt_mm, 0, 0, c)
                act.activation(yt[:, :], ps[:, c % 2, :], ACT.Identity, bias=vec[:, V_BS2:V_BS2 + 1]).then_inc(yt_done, 1)

            for k in range(16 + 8):
                if k < 16:
                    silu(k)
                if 2 <= k < 18:
                    h_high(k - 2)
                if k >= 8 and k % 4 == 0 and k // 4 - 2 < B:
                    sums(k // 4 - 2)

            def x_group(i, g):
                reach(act, tx_mm, i, 2, g + 1)
                reach(act, e_mm, i, TB, 4 * g - 4)
                act.activation(xg_hi[:, g % 2, :], ps[:, TX_ + g % 2, :], ACT.Copy).then_inc(xghi_done, 1)

            def silu_tile(i, k):
                reach(act, e_mm, i, TB, k + 1)
                reach(act, eh_done, i, TB, k - 1)
                act.activation(e_s[:, k % 2, :], ps[:, E_ + k % 2, 0:H], ACT.Silu).then_inc(esilu_done, 1)

            def hidden_high(i, k):
                reach(act, th_mm, i, TB, k + 1)
                reach(act, ey_mm, i, TB, k - 1)
                act.activation(e_hi[:, k % 2, :], ps[:, TH_ + k % 2, 0:H], ACT.Copy).then_inc(ehi_done, 1)

            def tiles_of(i, last=False):
                for k in range(TB):
                    silu_tile(i, k)
                    if k >= 1 or not first_of(i):
                        hidden_high(i, k - 1)
                    if k == 2:
                        x_group(i, 1)
                    if k == 6 and not last:
                        x_group(i, 2)

            x_group(0, 0)
            tiles_of(0)
            with act.Fori(1, TILES // TB - 1) as i:
                tiles_of(i)
            i = TILES // TB - 1
            tiles_of(i, last=True)
            hidden_high(i, TB - 1)

        @block.tensor
        def _(pe):
            def split_mm(out_ap, w_hi_ap, w_lo_ap, m_hi_ap, m_lo_ap, start=True, stop=True):
                pe.matmul(out_ap, w_hi_ap, m_hi_ap, start=start, stop=False)
                pe.matmul(out_ap, w_hi_ap, m_lo_ap, start=False, stop=False)
                return pe.matmul(out_ap, w_lo_ap, m_hi_ap, start=False, stop=stop)

            def turn_block(c):
                pe.wait_ge(xn_done, c + 1)
                for q in range(QT):
                    last = pe.transpose(ps[:, X_[c], P * q:P * q + P], xn[:, QT * c + q, :], ident)
                last.then_inc(xt_done, 1)

            pe.wait_ge(ld_c, 32)
            turn_block(0)

            def keys(b, m):
                reach(pe, ctx_split, b, 1, m // 4 + 1)
                reach(pe, qs_done, b, 4, m)
                w = slice(P * (m % 4), P * (m % 4) + P)
                split_mm(ps[:, Q_, 0:SKP], wk_hi[:, w], wk_lo[:, w], c_hi[:, 0:SKP], c_lo[:, 0:SKP]).then_inc(k_mm, 1)

            def queries(b, m):
                reach(pe, k_stack_done, b, 4, m + 1)
                tok = bass.ds(b * S + m // 4 * S, S)
                w = slice(P * (m % 4), P * (m % 4) + P)
                split_mm(ps[:, Q_, :], wq_hi[:, w], wq_lo[:, w], x_hi[:, tok], x_lo[:, tok]).then_inc(q_mm, 1)

            def values(b, nb):
                reach(pe, qmax_done, b, 4, 4 * nb)
                for a, w in enumerate((slice(0, P), slice(SKP, SKP + P))):
                    last = split_mm(ps[:, M_, D * a:D * a + D], c_hi[:, w], c_lo[:, w], wv_hi[:, :], wv_lo[:, :])
                last.then_inc(v_mm, 1)

            def score_rows(b, m, q):
                reach(pe, qs_done, b, 4, m + 1)
                reach(pe, ks_done, b, 16, 4 * m + 4)
                for a in range(2):
                    reach(pe, max_done, b, 32, 8 * m + 2 * q + a - 1)
                    o = ps[:, KS_ + a, 0:2 * SK].rearrange("p (c k) -> p c k", c=2)
                    h = HG * (m % 4) + 2 * a
                    pe.matmul(o, identb[:, :], mq_b[:, q:q + 1, :].to_broadcast([P, 2, SK]), start=True, stop=False)
                    pe.matmul(o, qs[0:96, m % 4, P * q:P * q + P], ks[0:96, h:h + 2, 0:SK],
                              start=False, stop=True).then_inc(smax_mm, 1)

            def turn_max(b, m):
                reach(pe, max_done, b, 32, 8 * m + 8)
                reach(pe, qmax_done, b, 4, m)
                reach(pe, v_done, b, 1, m // 4 + 1)
                for q in range(QT):
                    last = pe.transpose(ps[:, M_, P * q:P * q + P], mpad[:, m % 2, q, :], ident)
                last.then_inc(mt_mm, 1)

            def scores(b, m, t):
                n, g = 5 * m + t, m % 4
                reach(pe, exp_done, b, 20, n - 1)
                o = ps[:, ST_ + n % 2, :]
                if t == 0:
                    pe.matmul(o, repb[:, :, :], mkl_b[:, :], start=True, stop=False)
                    reach(pe, qmax_done, b, 4, m + 1)
                    reach(pe, ksl_done, b, 4, m + 1)
                    lhs = ksl[:, g, :, :]
                else:
                    pe.matmul(o, identb[:, :], mk_b[:, :], start=True, stop=False)
                    lhs = ks[:, HG * g + t - 1, 0:P]
                pe.matmul(o, lhs, qs[:, g, :], start=False, stop=True).then_inc(st_mm, 1)

            def weighted(b, m, t):
                n, g = 5 * m + t, m % 4
                reach(pe, exp_done, b, 20, 5 * m + (1, 5, 5, 5, 5)[t])
                if t == 0:
                    reach(pe, os_done, b, 4, m)
                    reach(pe, vx_done, b, 4, m + 1)
                    reach(pe, vl_done, b, 4, m + 1)
                    last = pe.matmul(ps[:, O_, :], vl[:, g, :, :], pf[:, n % RP, :], start=True, stop=False,
                                     skip_group_check=True)
                else:
                    j = t - 1
                    last = pe.matmul(ps[32 * j:32 * j + 32, O_, :], vx[:, HG * g + j, :], pf[:, n % RP, :],
                                     start=False, stop=True, skip_group_check=True)
                last.then_inc(pv_mm, 1)

            def turn_out(b, m):
                reach(pe, os_done, b, 4, m + 1)
                reach(pe, on_done, b, 4, m)
                if m % 4 == 0:
                    reach(pe, x1_done, b, 1, m // 4)
                if m % 4 == 1:
                    reach(pe, turned_lo, b, 1, m // 4)
                if m % 4 == 2:
                    reach(pe, lg_done, b, 1, m // 4)
                for q in range(QT):
                    last = pe.transpose(ps[:, T_, P * q:P * q + P], o_s[:, P * q:P * q + P], ident)
                last.then_inc(ot_mm, 1)

            def turn_normed(b, nb):
                reach(pe, normed, b, 1, nb + 1)
                if nb:
                    reach(pe, on_done, b, 4, 1)
                for q in range(QT):
                    last = pe.transpose(ps[:, T_, P * q:P * q + P], xn_b[:, q, :], ident)
                last.then_inc(turned_mm, 1)

            def logits(b, nb):
                reach(pe, turned_lo, b, 1, nb + 1)
                if nb:
                    reach(pe, on_done, b, 4, 2)
                tok = bass.ds((b + nb) * S, S)
                split_mm(ps[0:NE, T_, :], wg_hi[:, :], wg_lo[:, :], x_hi[:, tok], x_lo[:, tok]).then_inc(lgt_mm, 1)

            def turn_logits(b, nb):
                reach(pe, lgt_done, b, 1, nb + 1)
                apart(pe, pe_passed)
                for q in range(QT):
                    last = pe.transpose(ps[:, T_, NE * q:NE * q + NE], lgt[:, P * q:P * q + P], ident[0:NE, 0:NE])
                last.then_inc(lgt_turned, 1)

            def turn_batch(b, nb):
                reach(pe, on_done, b, 4, 4 * nb + 4)
                for q in range(QT):
                    last = pe.transpose(ps[:, T_, P * q:P * q + P], on[:, q, :], ident)
                last.then_inc(ont_mm, 1)

            def project(b, nb):
                reach(pe, ont_done, b, 1, nb + 1)
                for q in range(QT):
                    last = pe.matmul(ps[:, T_, P * q:P * q + P], on_t[:, P * q:P * q + P], wo_s[:, :],
                                     start=True, stop=True)
                last.then_inc(x1_mm, 1)

            def batch(b, last=False):
                for g in range(NG):
                    next1, next2 = not last or g + 1 < NG, not last or g + 2 < NG
                    scores(b, g, 2)
                    if next2:
                        keys(b, g + 2)
                    if next1:
                        score_rows(b, g + 1, 1)
                    if g == 3 and not last:
                        values(b, 1)
                    if g == 1 and not first_of(b):
                        turn_batch(b, -1)
                    if g == 3 and not first_of(b):
                        logits(b, -1)
                    scores(b, g, 3)
                    if next1:
                        score_rows(b, g + 1, 2)
                    if g == 1 and not first_of(b):
                        project(b, -1)
                    if g == 2 and not first_of(b):
                        turn_normed(b, -1)
                    if g == 3 and not first_of(b):
                        turn_logits(b, -1)
                    scores(b, g, 4)
                    if next1:
                        score_rows(b, g + 1, 3)
                    if next2:
                        queries(b, g + 2)
                    if next1:
                        turn_max(b, g + 1)
                    weighted(b, g, 0)
                    if g or not first_of(b):
                        turn_out(b, g - 1)
                    if next1:
                        scores(b, g + 1, 0)
                        scores(b, g + 1, 1)
                    for t in range(1, 5):
                        weighted(b, g, t)
                    if next2:
                        score_rows(b, g + 2, 0)

            pe.wait_ge(xlo_done, 1)
            pe.wait_ge(consts_done, 1)
            keys(0, 0)
            turn_block(1)
            turn_block(2)
            queries(0, 0)
            turn_block(3)
            score_rows(0, 0, 0)
            keys(0, 1)
            score_rows(0, 0, 1)
            queries(0, 1)
            score_rows(0, 0, 2)
            values(0, 0)
            score_rows(0, 0, 3)
            turn_max(0, 0)
            pe.wait_ge(xlo_done, B)
            scores(0, 0, 0)
            scores(0, 0, 1)
            score_rows(0, 1, 0)
            batch(0)
            with pe.Fori(1, B - 1) as b:
                batch(b)
            batch(B - 1, last=True)
            turn_out(B - 1, NG - 1)
            turn_batch(B - 1, 0)
            project(B - 1, 0)

            turn_normed(B - 1, 0)
            logits(B - 1, 0)
            turn_logits(B - 1, 0)

            def first(k):
                reach(pe, silu_done, 0, 0, k - 1)
                reach(pe, h_done, 0, 0, k - 1)
                e, u, tok = k % 4 // 2, k % 2, slice(k // 4 * S, k // 4 * S + S)
                for m, done in ((0, a_mm), (1, b_mm)):
                    cols = slice(H * m + P * u, H * m + P * u + P)
                    split_mm(ps[:, AB_ + 2 * (k % 2) + m, :], w[:, e, 0, cols], w[:, e, 1, cols], x_hi[:, tok],
                             x_lo[:, tok]).then_inc(done, 1)

            def second(k):
                pe.wait_ge(hlo_done, k + 1)
                c, e = k // 4, k % 4 // 2
                if k % 4 == 0:
                    reach(pe, x2_done, 0, 0, c - 1)
                cols = slice(2 * H + P * (k % 2), 2 * H + P * (k % 2) + P)
                last = split_mm(ps[:, c % 2, :], w[:, e, 0, cols], w[:, e, 1, cols], h_hi[:, k % 4, :], h_lo[:, k % 4, :],
                                start=k % 4 == 0, stop=k % 4 == 3)
                last.then_inc(w2_mm, 1)

            def turn_sums(c):
                pe.wait_ge(yt_done, c + 1)
                for q in range(QT):
                    last = pe.transpose(ps[:, c % 2, P * q:P * q + P], yt[:, P * q:P * q + P], ident)
                last.then_inc(ytt_mm, 1)

            def rank_rows():
                pe.wait_ge(sel_done, 1)
                picks = sel[:, :, :].rearrange("p t e -> p (t e)")
                pe.matmul(ps[:, CNT_, 0:NT * NE], one_b[:, :], picks, start=True, stop=True)
                pe.matmul(ps[:, RANK_, 0:NT * NE], up_b[:, :], picks, start=True, stop=True, skip_group_check=True)
                for t in range(NT - 1):
                    n = NT - 1 - t
                    last = pe.matmul(ps[:, RANK_, NE * (t + 1):NT * NE].rearrange("p (a e) -> p a e", e=NE), one_b[:, :],
                                     sel[:, t:t + 1, :].to_broadcast([P, n, NE]), start=False, stop=True,
                                     skip_group_check=True)
                last.then_inc(rank_mm, 1)

            first(0)
            pe.wait_ge(lg_done, B)
            first(1)
            rank_rows()
            for k in range(2, 16 + LAG + 2):
                if k < 16:
                    first(k)
                if LAG <= k < 16 + LAG:
                    second(k - LAG)
                if 9 <= k < 21 and k % 4 == 1:
                    turn_sums((k - 9) // 4)

            def expert_of(n):
                return pe.value_load(te[0:1, n:n + 1], min_val=NX - NE, max_val=NX - 1)

            def tile_biases(n, out_ap, cols, start):
                pe.matmul(out_ap, tile_one[:, n:n + 1].to_broadcast([NB, P]), b_all[:, cols], start=start, stop=False)

            def weights(e, part, cols):
                return w[:, bass.ds(e, 1), part, cols].rearrange("p a n -> p (a n)")

            def turn_rows(g):
                pe.wait_ge(ld_g[g % 2], 16 + 16 * (g // 2))
                if g == 1:
                    pe.wait_ge(x2_done, B)
                reach(pe, xglo_done, 0, 0, g - 1)
                for j in range(4):
                    last = pe.transpose(ps[:, TX_ + g % 2, P * j:P * j + P], xg[:, g % 2, j, 0:D], ident)
                last.then_inc(tx_mm, 1)

            def up(n, e):
                g = n // 4
                pe.wait_ge(xglo_done, g + 1)
                reach(pe, eh_done, 0, 0, n - 1)
                o = ps[:, E_ + n % 2, :]
                tile_biases(n, o, slice(0, 2 * H), start=True)
                hi, lo = (v[:, g % 2, P * (n % 4):P * (n % 4) + P] for v in (xg_hi, xg_lo))
                split_mm(o, hi, lo, weights(e, 0, slice(0, 2 * H)), weights(e, 1, slice(0, 2 * H)),
                         start=False).then_inc(e_mm, 1)

            def turn_hidden(n):
                pe.wait_ge(eh_done, n + 1)
                reach(pe, elo_done, 0, 0, n - 1)
                for c in range(2):
                    last = pe.transpose(ps[:, TH_ + n % 2, P * c:P * c + P], e_h[:, n % 2, P * c:P * c + P], ident)
                last.then_inc(th_mm, 1)

            def down(n, e):
                pe.wait_ge(elo_done, n + 1)
                reach(pe, yo_done, 0, 0, n - 1)
                both, o = ps[:, Y_ + n % 2, 0:2 * D], ps[:, Y_ + n % 2, 0:D]
                (hi0, lo0), (hi1, lo1) = ([v[:, n % 2, P * c:P * c + P] for v in (e_hi, e_lo)] for c in range(2))
                c0, c1 = (slice(2 * H + D * c, 2 * H + D * c + D) for c in range(2))

                def parts(cols):
                    return w[:, bass.ds(e, 1), :, cols].rearrange("p a s n -> p (a s) n")

                pe.matmul(both.rearrange("p (s n) -> p s n", s=2), hi0, parts(c0), start=True, stop=False)
                tile_biases(n, o, slice(2 * H, BW), start=False)
                pe.matmul(o, lo0, weights(e, 0, c0), start=False, stop=False)
                pe.matmul(o, lo1, weights(e, 0, c1), start=False, stop=False)
                last = pe.matmul(both.rearrange("p (s n) -> p s n", s=2), hi1, parts(c1), start=False, stop=True)
                last.then_inc(ey_mm, 1)

            pe.wait_ge(x2_done, B - 1)
            turn_rows(0)
            turn_sums(B - 1)
            pe.wait_ge(tile_known, 1)
            pe.wait_ge(w_split, 2 * NX)
            pe.wait_ge(b_step, 10)
            experts = {0: expert_of(0)}
            for n in range(TILES + 2):
                if n % 4 == 1 and n // 4 + 1 < TILES // 4:
                    turn_rows(n // 4 + 1)
                if n < TILES:
                    up(n, experts[n])
                if n + 1 < TILES:
                    experts[n + 1] = expert_of(n + 1)
                if 1 <= n <= TILES:
                    turn_hidden(n - 1)
                if n >= 2:
                    down(n - 2, experts.pop(n - 2))


def constants():
    import numpy as np
    c = np.zeros((P, C_END), np.float32)
    p = np.arange(P)
    c[:, C_ID:C_ID + P] = np.eye(P)
    c[:, C_MQ] = p // 32 == 1
    c[:, C_MK] = p // 32 == 2
    for j in range(HG):
        c[:, C_SELM + j] = (p < 96) & ((p % 32) // DK == j)
        c[:, C_SELO + j] = p == 96 + j
    c[:, C_EPS] = EPS
    for j in range(HG):
        c[:, C_QUAD + j] = p // 32 == j
    c[:, C_DESC:C_DESC + NE] = NE - np.arange(NE)
    c[:, C_UP:C_UP + P] = p[:, None] < p[None, :]
    e = np.arange(NE)
    c[:, C_T128:C_T128 + NE] = P * e
    c[:, C_LT:C_LT + NE * NE] = (e[None, :] < e[:, None]).reshape(1, -1)
    c[:, C_TILE:C_TILE + TILES] = np.arange(TILES)
    c[:, C_SPARE:C_SPARE + TILES] = 2 * TOK + P * np.arange(TILES) + p[:, None]
    for k in range(2):
        c[:, C_DEST + NT * k:C_DEST + NT * k + NT] = k * TOK + P * np.arange(NT) + p[:, None] - 2 * TOK
    for r in range(3):
        c[:, C_PART + r] = p // NE == r
    c[:, C_EXP:C_EXP + NE] = p[:, None] % NE == e
    return c


def kernel(x, ctx_1024, mask_SxS2_ik0, L0_xattn_Wq, L0_xattn_bq, L0_xattn_Wk, L0_xattn_bk, L0_xattn_Wv, L0_xattn_bv,
           L0_xattn_Wo, L0_xattn_bo, L0_ffn_Wg, L0_ffn_W1, L0_ffn_b1, L0_ffn_W11, L0_ffn_b11, L0_ffn_W2, L0_ffn_b2,
           L0_ffn_Ws1, L0_ffn_bs1, L0_ffn_Ws11, L0_ffn_bs11, L0_ffn_Ws2, L0_ffn_bs2):
    import numpy as np
    import concourse.bacc as bacc
    from concourse.bass_utils import run_bass_kernel_spmd

    def stacked(w):
        return np.tile(np.asarray(w).T.reshape(D, NG, 1, 32), (1, 1, 4, 1)).reshape(D, NG * P)

    def stacked_bias(v):
        return np.tile(np.asarray(v).reshape(NG, 1, 32), (1, 4, 1)).reshape(NG, P).T

    def halves(w):
        return np.stack([w[..., 0:H], w[..., H:2 * H]])

    ctx_t = np.zeros((D, B, CW), np.float32)
    c = np.asarray(ctx_1024).transpose(2, 0, 1)
    ctx_t[:, :, 0:SK] = c
    for j in range(HG):
        ctx_t[:, :, SKP + 32 * j:SKP + 32 * j + SK - P] = c[:, :, P:SK]
    mask = np.asarray(mask_SxS2_ik0)
    mask_kl = np.zeros((32, S), mask.dtype)
    mask_kl[0:SK - P] = mask.T[P:SK]
    w1 = np.concatenate([halves(L0_ffn_Ws1), L0_ffn_W1])
    w11 = np.concatenate([halves(L0_ffn_Ws11), L0_ffn_W11])
    w2 = np.concatenate([np.asarray(L0_ffn_Ws2).reshape(2, H, D), L0_ffn_W2])
    w2 = w2.reshape(NX, 2, P, D).transpose(0, 2, 1, 3).reshape(NX, P, 2 * D)
    b1 = np.concatenate([halves(L0_ffn_bs1), L0_ffn_b1]).reshape(NX * 2, P).T
    b11 = np.concatenate([halves(L0_ffn_bs11), L0_ffn_b11]).reshape(NX * 2, P).T
    arrays = {
        "x": np.asarray(x).reshape(NT, P, D).transpose(1, 0, 2),
        "ctx_t": ctx_t,
        "wq": stacked(L0_xattn_Wq),
        "wk": stacked(L0_xattn_Wk),
        "wv": np.asarray(L0_xattn_Wv).T,
        "wo": np.asarray(L0_xattn_Wo).T,
        "mask_q": mask.reshape(QT, P, SK).transpose(1, 0, 2),
        "mask_k": mask.T[0:P],
        "mask_kl": mask_kl,
        "bias_cols": np.concatenate([stacked_bias(L0_xattn_bq), stacked_bias(L0_xattn_bk), b1, b11,
                                     np.asarray(L0_ffn_bs2)[:, None]], axis=1),
        "bv_rows": np.tile(np.asarray(L0_xattn_bv), (P, 1)),
        "bo_rows": np.tile(np.asarray(L0_xattn_bo), (P, 1)),
        "wg": L0_ffn_Wg,
        "b_rows": np.tile(np.concatenate([L0_ffn_b1, L0_ffn_b11, L0_ffn_b2], axis=1), (3, 1)),
        "w_ffn": np.concatenate([w1, w11, w2], axis=2),
        "consts": constants(),
    }
    arrays = {name: np.ascontiguousarray(a) for name, a in arrays.items()}
    nc = bacc.Bacc("TRN2", target_bir_lowering=False, num_devices=1)
    aps = [nc.dram_tensor(name, a.shape, mybir.dt.from_np(a.dtype), kind="ExternalInput").ap()
           for name, a in arrays.items()]
    out = nc.dram_tensor("out", (P, NT, D), F32, kind="ExternalOutput").ap()
    build(nc, *aps, out)
    r = run_bass_kernel_spmd(nc, [arrays], core_ids=[0])
    return r.results[0]["out"].transpose(1, 0, 2).reshape(B, S, D)
```
